# Optimizing a Trainium2 kernel written in Bass

```python
import numpy as np
import jax
import jax.numpy as jnp

def _softmax(x, axis=-1):
    return jax.nn.softmax(x, axis=axis)

def _gelu(x):
    return jax.nn.gelu(x, approximate=True)

def _silu(x):
    return jax.nn.silu(x)

def _sigmoid(x):
    return jax.nn.sigmoid(x)

def _layernorm(x, axis=-1, eps=1e-05):
    m = jnp.mean(x, axis=axis, keepdims=True)
    v = jnp.var(x, axis=axis, keepdims=True)
    return (x - m) / jnp.sqrt(v + eps)

def _scatter_add(tgt, idx, src, axis=0):
    return tgt.at[idx].add(src)

def _segment_sum(src, seg, n):
    return jax.ops.segment_sum(src, seg, n)
kernel_name = 'mk_gnn_preln_d2_gnn_r8_5c1c8e'

def setup_inputs(seed: int=0):
    np.random.seed(seed)
    _w = jnp.asarray

    def _rec_inputs():
        import jax
        import jax.numpy as jnp
        _gk = jax.random.key(seed)
        x = -0.000202 + 1 * jax.random.normal(jax.random.fold_in(_gk, 1), (12500, 128), jnp.float32)
        src = jax.random.randint(jax.random.fold_in(_gk, 2), (200000,), 0, 12500, jnp.int32)
        dst = jax.random.randint(jax.random.fold_in(_gk, 3), (200000,), 0, 12500, jnp.int32)
        _o = jnp.argsort(dst, stable=True)
        src = src[_o]
        dst = dst[_o]
        edge_weight1 = jax.random.uniform(jax.random.fold_in(_gk, 12), (200000, 1), jnp.float32, 0.0, 0.999998)
        return (x, src, dst, edge_weight1)
    x, src, dst, edge_weight1 = _rec_inputs()

    def _L0_gnn_setup():
        import jax, jax.numpy as jnp
        import numpy as np
        N_NODES = 6250
        N_EDGES = 100000
        IN_DIM = 128
        OUT_DIM = 128
        NEG_SLOPE = 0.2
        key = jax.random.key(seed)
        k1, k2, k3, k4, k5 = jax.random.split(key, 5)
        x = jax.random.normal(k1, (N_NODES, IN_DIM), dtype=jnp.float32)
        edge_index = jax.random.randint(k2, (2, N_EDGES), 0, N_NODES, dtype=jnp.int64)
        W = jax.random.normal(k3, (IN_DIM, OUT_DIM), dtype=jnp.float32) * (1.0 / np.sqrt(IN_DIM))
        a_src = jax.random.normal(k4, (OUT_DIM,), dtype=jnp.float32) * (1.0 / np.sqrt(OUT_DIM))
        a_dst = jax.random.normal(k5, (OUT_DIM,), dtype=jnp.float32) * (1.0 / np.sqrt(OUT_DIM))
        bias = jnp.zeros((OUT_DIM,), dtype=jnp.float32)
        return {'x': x, 'edge_index': edge_index, 'W': W, 'a_src': a_src, 'a_dst': a_dst, 'bias': bias}
    _L0_gnn_all = _L0_gnn_setup()
    _L0_gnn_in = {k: v for k, v in _L0_gnn_all.items() if k in ('W', 'a_src', 'a_dst', 'bias')}
    del _L0_gnn_all

    def _L1_gnn_setup():
        import jax, jax.numpy as jnp
        import numpy as np
        N_NODES = 5000
        key = jax.random.key(seed)
        k1, k2, k3, k4, k5 = jax.random.split(key, 5)
        x = jax.random.normal(k1, (N_NODES, 128), dtype=jnp.float32)
        edge_index = jax.random.randint(k2, (2, 80000), 0, N_NODES, dtype=jnp.int64)
        edge_attr = jax.random.uniform(k3, (80000, 1), dtype=jnp.float32)
        weight = jax.random.normal(k4, (256, 128), dtype=jnp.float32) * 0.05
        bias = jax.random.normal(k5, (128,), dtype=jnp.float32) * 0.05
        return {'x': x, 'edge_index': edge_index, 'edge_attr': edge_attr, 'weight': weight, 'bias': bias}
    _L1_gnn_all = _L1_gnn_setup()
    _L1_gnn_in = {k: v for k, v in _L1_gnn_all.items() if k in ('weight', 'bias')}
    del _L1_gnn_all
    return {'x': x, 'src': src, 'dst': dst, 'edge_weight1': edge_weight1, 'L0_gnn_W': _L0_gnn_in['W'], 'L0_gnn_a_src': _L0_gnn_in['a_src'], 'L0_gnn_a_dst': _L0_gnn_in['a_dst'], 'L0_gnn_bias': _L0_gnn_in['bias'], 'L1_gnn_weight': _L1_gnn_in['weight'], 'L1_gnn_bias': _L1_gnn_in['bias']}

def reference(x, src, dst, edge_weight1, L0_gnn_W, L0_gnn_a_src, L0_gnn_a_dst, L0_gnn_bias, L1_gnn_weight, L1_gnn_bias):
    import jax
    import jax.numpy as jnp

    def _L0_gnn_ref(x, edge_index, W, a_src, a_dst, bias):
        import jax, jax.numpy as jnp
        import numpy as np
        N_NODES = 6250
        N_EDGES = 100000
        IN_DIM = 128
        OUT_DIM = 128
        NEG_SLOPE = 0.2
        N = x.shape[0]
        h = x @ W
        src, dst = (edge_index[0], edge_index[1])
        e_src = h @ a_src
        e_dst = h @ a_dst
        raw = jax.nn.leaky_relu(e_src[src] + e_dst[dst], negative_slope=NEG_SLOPE)
        per_recv_max = jax.ops.segment_max(raw, dst, num_segments=N)
        per_recv_max = jnp.where(jnp.isfinite(per_recv_max), per_recv_max, jnp.zeros_like(per_recv_max))
        exp = jnp.exp(raw - per_recv_max[dst])
        denom = jnp.maximum(jax.ops.segment_sum(exp, dst, num_segments=N), 1e-15)
        alpha = exp / denom[dst]
        msg = h[src] * alpha[:, None]
        agg = jax.ops.segment_sum(msg, dst, num_segments=N)
        return jax.nn.elu(agg + bias)

    def _L1_gnn_ref(x, edge_index, edge_attr, weight, bias):
        import jax, jax.numpy as jnp
        import numpy as np
        N_NODES = 5000
        row, col = (edge_index[0], edge_index[1])
        num_nodes = x.shape[0]
        alpha = jnp.concatenate([x[row], x[col]], axis=-1)
        alpha = alpha @ weight
        alpha = edge_attr * alpha
        sums = jax.ops.segment_sum(alpha, row, num_segments=num_nodes)
        counts = jax.ops.segment_sum(jnp.ones((alpha.shape[0],), dtype=alpha.dtype), row, num_segments=num_nodes)
        out = sums / jnp.maximum(counts, 1.0)[:, None]
        return out + bias
    edge_index = jnp.stack([src, dst])
    h = jnp.maximum(_layernorm(x, axis=-1), 0.0)
    x = x + _L0_gnn_ref(h, edge_index, L0_gnn_W, L0_gnn_a_src, L0_gnn_a_dst, L0_gnn_bias)
    h = jnp.maximum(_layernorm(x, axis=-1), 0.0)
    x = x + _L1_gnn_ref(h, edge_index, edge_weight1, L1_gnn_weight, L1_gnn_bias)
    return x

_drawn_inputs = setup_inputs


def setup_inputs(seed=0):
    import zlib

    import numpy as np

    out = dict(_drawn_inputs(seed))
    spreads = {'L0_gnn_bias': (0.0, 0.1)}
    factors = {'L0_gnn_a_dst': 8.0}
    for name, (base, spread) in spreads.items():
        noise = np.random.default_rng([zlib.crc32(name.encode()), seed]).standard_normal(out[name].shape)
        drawn = base * np.exp(spread * noise) if base else spread * noise
        out[name] = jnp.asarray(drawn.astype(out[name].dtype))
    for name, factor in factors.items():
        out[name] = (out[name] * factor).astype(out[name].dtype)
    return out
```

```python
from contextlib import ExitStack

import numpy as np

import concourse.bass as bass
from concourse import mybir

F32 = mybir.dt.float32
BF16 = mybir.dt.bfloat16
I32 = mybir.dt.int32
I16 = mybir.dt.int16
ALU = mybir.AluOpType
ACT = mybir.ActivationFunctionType
X = mybir.AxisListType.X

P = 128
N = 12500
E = 200000
D = 128
NB = -(-N // P)
NP = NB * P
W = 128
GT = 8
T = 1568
EP = T * P
NG = T // GT
TR = T - 12 * P
PIECES = [(k, P) for k in range(12)] + [(12, TR)]
CB = 7
NC = NB // CB
CW = CB * P
AW = NP + W
NACC = 4
RW = D + 2
BIG = 1e30
EPS = 1e-5
SLOPE = 0.2

C_ID, C_IOTA, C_ROW0, C_PART, C_U0, C_U1, C_T0, C_T1, C_TRASH, C_EPS, C_TRI, C_ONES = (
    0, 128, 256, 384, 385, 386, 387, 388, 389, 390, 391, 519)
C_WIDTH = 647


def shape_constants():
    c = np.zeros((P, C_WIDTH), np.float32)
    p = np.arange(P)
    c[:, C_ID:C_ID + P] = np.eye(P)
    c[:, C_IOTA:C_IOTA + P] = p[None, :]
    c[0, C_ROW0:C_ROW0 + P] = 1.0
    c[:, C_PART] = p
    power = 4.0 ** (32 - p % 64)
    low = p < 64
    c[:, C_U0] = np.where(low, power, 0.0)
    c[:, C_U1] = np.where(low, 0.0, power)
    c[:, C_T0] = np.where(low, 2 * power, 4.0 ** -32)
    c[:, C_T1] = np.where(low, BIG, 2 * power)
    c[:, C_TRASH] = NP + p
    c[:, C_EPS] = EPS
    c[:, C_TRI:C_TRI + P] = (p[:, None] < p[None, :])
    c[:, C_ONES:C_ONES + P] = 1.0
    return c


def build(nc, x, src, dst, weight, w0, a_src, a_dst, bias0, w1, bias1, consts, out):
    def dram(name, shape, dt):
        return nc.dram_tensor(name, shape, dt, kind="Internal").ap()

    src_flat = dram("src_flat", (EP,), I32)
    dst_flat = dram("dst_flat", (EP,), I32)
    wgt_flat = dram("wgt_flat", (EP,), F32)
    lo_src_flat = dram("lo_src_flat", (EP,), BF16)
    lo_dst_flat = dram("lo_dst_flat", (EP,), BF16)
    src16_flat = dram("src16_flat", (EP,), I16)
    es_flat = dram("es_flat", (EP,), F32)
    ed_flat = dram("ed_flat", (EP,), F32)
    alpha_flat = dram("alpha_flat", (EP,), F32)
    h_table = dram("h_table", (NP, D), F32)
    h2_table = dram("h2_table", (AW, D), F32)
    acc = [dram(f"acc{k}", (AW, RW), F32) for k in range(NACC)]

    whole = ExitStack()

    def sb(stack, name, shape, dt=F32):
        return stack.enter_context(nc.sbuf_tensor(name, shape, dt))

    def ps(stack, name, shape, dt=F32):
        return stack.enter_context(nc.psum_tensor(name, shape, dt))

    def sem(name):
        return whole.enter_context(nc.semaphore(name))

    passed = sem("passed")

    def hold(eng, semaphore, value):
        eng.wait_ge(semaphore, value)
        eng.sem_inc(passed, 1)

    class Chain:

        def __init__(self, eng, name):
            self.eng, self.sem, self.n = eng, sem(name), 0

        def __call__(self, instruction):
            self.n += 1
            instruction.then_inc(self.sem, 1)
            self.eng.wait_ge(self.sem, self.n)

    with whole:
        con = sb(whole, "con", [P, C_WIDTH])
        ident = con[:, C_ID:C_ID + P]
        iota = con[:, C_IOTA:C_IOTA + P]
        x_sb = sb(whole, "x_sb", [P, NB, D])
        src_c = sb(whole, "src_c", [P, T])
        dl = sb(whole, "dl", [P, T])
        r4 = sb(whole, "r4", [P, T, 4])
        base_i = sb(whole, "base_i", [1, NG], I32)
        passes = sb(whole, "passes", [1, 1], I32)
        bias0_col = sb(whole, "bias0_col", [P, 1])

        to_layer1 = ExitStack()
        src_i = sb(to_layer1, "src_i", [P, T], I32)
        alpha = sb(to_layer1, "alpha", [P, T])
        wext = sb(to_layer1, "wext", [P, D + 2])
        es_tab = sb(to_layer1, "es_tab", [P, NB])
        ed_tab = sb(to_layer1, "ed_tab", [P, NB])
        dst_c = sb(to_layer1, "dst_c", [P, T])
        hi_src = sb(to_layer1, "hi_src", [P, T])
        hi_dst = sb(to_layer1, "hi_dst", [P, T])

        s_copied = sem("edges_copied")
        s_con = sem("constants_loaded")
        s_x = sem("x_loaded")
        s_xz = sem("x_padding_zeroed")
        s_zero = sem("zeros_written")
        s_zt = sem("zero_tile")
        zs = ExitStack()
        zero_tile = sb(zs, "zero_tile", [P, AW * RW // P // 10])
        block = nc.Block()
        with block:
            @block.sync
            def _(sp):
                sp.dma_start(con[:], consts).then_inc(s_con, 16)
                for a, b in ((src_flat, src), (dst_flat, dst), (wgt_flat, weight)):
                    sp.dma_start(a[0:E].rearrange("(a b) -> a b", a=P // 2),
                                 b[0:E].rearrange("(a b) -> a b", a=P // 2)).then_inc(s_copied, 16)
                for a, b in ((src_flat, src), (dst_flat, dst)):
                    sp.dma_start(a[E:EP].rearrange("(a b) -> a b", b=1),
                                 b[E - 1:E].partition_broadcast(EP - E)).then_inc(s_copied, 16)
                sp.wait_ge(s_xz, 1)
                sp.dma_start(x_sb[:, 0:NB - 1, :],
                             x[0:(NB - 1) * P, :].rearrange("(b p) f -> p b f", p=P)).then_inc(s_x, 16)
                sp.dma_start(x_sb[0:N - (NB - 1) * P, NB - 1, :], x[(NB - 1) * P:N, :]).then_inc(s_x, 16)
                sp.wait_ge(s_zt, 1)
                sp.dma_start(wgt_flat[E:EP].rearrange("(a b) -> a b", a=1),
                             zero_tile[0:1, 0:EP - E]).then_inc(s_copied, 16)
                n = AW * RW // P
                for k in range(NACC):
                    view = acc[k].rearrange("r c -> (r c)").rearrange("(p m) -> p m", p=P)
                    for j in range(10):
                        sp.dma_start(view[:, j * (n // 10):(j + 1) * (n // 10)],
                                     zero_tile[:, :]).then_inc(s_zero, 16)
                sp.dma_start(h2_table[NP:AW, :], zero_tile[:, 0:D]).then_inc(s_zero, 16)
                sp.wait_ge(s_con, 16)
                sp.wait_ge(s_copied, 96)
                sp.wait_ge(s_x, 32)
                sp.wait_ge(s_zero, 16 * (10 * NACC + 1))

            @block.vector
            def _(dve):
                dve.memset(x_sb[:, NB - 1, :], 0.0).then_inc(s_xz, 1)
                dve.memset(zero_tile[:], 0.0).then_inc(s_zt, 1)
        zs.close()

        st = ExitStack()
        rows_i = sb(st, "rows_i", [P, 13, P], I32)
        rows_f = sb(st, "rows_f", [P, 13, P])
        tmp_i = sb(st, "tmp_i", [P, T], I32)
        lo_b = sb(st, "lo_b", [P, T], BF16)
        lo_h = sb(st, "lo_h", [P, T], I16)
        wide = sb(st, "wide", [1, NG])
        wide1 = sb(st, "wide1", [1, 2])
        base_b = sb(st, "base_b", [P, NG])
        last = sb(st, "last", [P, NG])
        ps_t = ps(st, "ps_t", [P, 4, 512])
        ps_b = ps(st, "ps_b", [P, 512])
        cols = ps_t[:, :, :].rearrange("p a b -> p (a b)")[:, 0:T]
        s_rows = sem("rows_loaded")
        s_rowf = sem("rows_as_floats")
        s_cols = sem("rows_transposed")
        s_free = sem("columns_copied")
        s_flat = sem("flat_loaded")
        s_lo = sem("low_bits_ready")
        s_los = sem("low_bits_stored")
        s_base = sem("bases_broadcast")

        def load_rows(sp, tile, flat, semaphore):
            sp.dma_start(tile[:, 0:12, :],
                         flat[0:12 * P * P].rearrange("(k r e) -> r k e", k=12, r=P)).then_inc(semaphore, 16)
            sp.dma_start(tile[0:TR, 12, :],
                         flat[12 * P * P:EP].rearrange("(r e) -> r e", r=TR)).then_inc(semaphore, 16)

        def transpose_rows(pe, rows, columns, done):
            for k, r in PIECES:
                last_one = pe.transpose(columns[:, k * P:k * P + r], rows[0:r, k, :], ident[0:r, 0:r])
            last_one.then_inc(done, 1)

        block = nc.Block()
        with block:
            @block.sync
            def _(sp):
                load_rows(sp, rows_i, src_flat, s_rows)
                sp.wait_ge(s_rowf, 1)
                load_rows(sp, rows_i, dst_flat, s_rows)
                sp.wait_ge(s_free, 2)
                load_rows(sp, rows_f, wgt_flat, s_rows)
                for n, flat in enumerate((src_flat, dst_flat)):
                    sp.wait_ge(s_free, 3 + n)
                    sp.dma_start(tmp_i[:], flat.rearrange("(p m) -> p m", p=P)).then_inc(s_flat, 16)
                    sp.wait_ge(s_lo, n + 1)
                    sp.dma_start((lo_src_flat, lo_dst_flat)[n].rearrange("(p m) -> p m", p=P),
                                 lo_b[:]).then_inc(s_los, 16)
                    if n == 0:
                        sp.dma_start(src16_flat.rearrange("(p m) -> p m", p=P), lo_h[:]).then_inc(s_los, 16)
                sp.wait_ge(s_los, 48)

            @block.vector
            def _(dve):
                link = Chain(dve, "edge_chain")
                for n, (as_float, hi) in enumerate(((src_c, hi_src), (dst_c, hi_dst))):
                    dve.wait_ge(s_rows, 32 * (n + 1))
                    if n:
                        dve.wait_ge(s_cols, n)
                    dve.tensor_copy(rows_f[:, 0:12, :], rows_i[:, 0:12, :])
                    dve.tensor_copy(rows_f[0:TR, 12, :], rows_i[0:TR, 12, :]).then_inc(s_rowf, 1)
                    dve.wait_ge(s_cols, n + 1)
                    dve.tensor_copy(as_float[:], cols)
                    ints = src_i if n == 0 else tmp_i
                    link(dve.tensor_copy(ints[:], cols))
                    link(dve.tensor_scalar(tmp_i[:], ints[:], 7, None, ALU.arith_shift_right))
                    link(dve.tensor_copy(hi[:], tmp_i[:]))
                    dve.sem_inc(s_free, 1)
                dve.wait_ge(s_cols, 3)
                dve.tensor_copy(r4[:, :, 0], cols)
                dve.memset(r4[:, 0:E // P, 1], 1.0)
                link(dve.memset(r4[:, E // P:T, 1], 0.0))
                dve.memset(r4[0:E % P, E // P, 1:2], 1.0)
                dve.memset(r4[:, :, 2:4], 1.0)
                dve.wait_ge(s_base, 2)
                link(dve.tensor_copy(base_b[:], ps_b[:, 0:NG]))
                grouped = dl[:, :].rearrange("p (g j) -> p g j", j=GT)
                link(dve.tensor_tensor(grouped, dst_c[:, :].rearrange("p (g j) -> p g j", j=GT),
                                       base_b[:, :].unsqueeze(2).broadcast_to([P, NG, GT]), ALU.subtract))
                dve.tensor_copy(base_i[:], base_b[0:1, :])
                for k in (2, 3):
                    link(dve.tensor_scalar(r4[:, :, k], r4[:, :, k], con[:, C_U0 + k - 2:C_U0 + k - 1], None,
                                           ALU.mult))
                link(dve.tensor_tensor(wide[:], ps_b[0:1, NG:2 * NG], base_b[0:1, :], ALU.subtract))
                link(dve.tensor_reduce(wide1[:, 0:1], wide[:], X, ALU.max))
                link(dve.tensor_copy(tmp_i[0:1, 0:1], wide1[:, 0:1]))
                link(dve.tensor_scalar(tmp_i[0:1, 0:1], tmp_i[0:1, 0:1], 7, None, ALU.arith_shift_right))
                link(dve.tensor_copy(wide1[:, 0:1], tmp_i[0:1, 0:1]))
                link(dve.tensor_scalar(passes[:], wide1[:, 0:1], 1.0, None, ALU.add))
                dve.sem_inc(s_free, 1)
                for n in range(2):
                    dve.wait_ge(s_flat, 16 * (n + 1))
                    if n:
                        dve.wait_ge(s_los, 32)
                    if n == 0:
                        dve.tensor_copy(lo_h[:], tmp_i[:])
                    link(dve.tensor_scalar(tmp_i[:], tmp_i[:], 127, None, ALU.bitwise_and))
                    link(dve.tensor_copy(lo_b[:], tmp_i[:]))
                    dve.sem_inc(s_free, 1)
                    dve.sem_inc(s_lo, 1)

            @block.tensor
            def _(pe):
                for n in range(3):
                    if n < 2:
                        pe.wait_ge(s_rowf, n + 1)
                    else:
                        pe.wait_ge(s_rows, 96)
                    if n:
                        pe.wait_ge(s_free, n)
                    transpose_rows(pe, rows_f, cols, s_cols)
                ends = dst_c[:, :].rearrange("p (g j) -> p g j", j=GT)
                pe.matmul(ps_b[:, 0:NG], con[:, C_ROW0:C_ROW0 + P], ends[:, :, 0],
                          start=True, stop=True).then_inc(s_base, 1)
                pe.matmul(ps_b[0:1, NG:2 * NG], con[:, C_ID + P - 1:C_ID + P], ends[:, :, GT - 1],
                          start=True, stop=True).then_inc(s_base, 1)
        st.close()

        def norm_vector(dve, i, xin, t, s):
            hold(dve, s["in"], i + 1) if s["in"] is not None else None
            dve.tensor_reduce(t["mean"][:], xin, X, ALU.add).then_inc(s["chain"], 1)
            dve.wait_ge(s["chain"], i * 3 + 1)
            dve.tensor_scalar(t["mean"][:], t["mean"][:], -1.0 / D, None, ALU.mult).then_inc(s["chain"], 1)
            dve.wait_ge(s["chain"], i * 3 + 2)
            dve.tensor_tensor(t["xc"][:], xin, t["mean"][:, :].unsqueeze(2).broadcast_to([P, CB, D]),
                              ALU.add).then_inc(s["centred"], 1)
            hold(dve, s["squared"], i + 1)
            dve.tensor_reduce(t["var"][:], t["sq"][:], X, ALU.add).then_inc(s["summed"], 1)
            hold(dve, s["rooted"], i + 1)
            dve.reciprocal(t["std"][:], t["std"][:]).then_inc(s["chain"], 1)
            dve.wait_ge(s["chain"], i * 3 + 3)

        def norm_scalar(act, i, t, s):
            act.wait_ge(s["centred"], i + 1)
            act.activation(t["sq"][:], t["xc"][:], ACT.Square).then_inc(s["squared"], 1)
            act.wait_ge(s["summed"], i + 1)
            act.activation(t["std"][:], t["var"][:], ACT.Sqrt, bias=con[:, C_EPS:C_EPS + 1],
                           scale=1.0 / D).then_inc(s["rooted"], 1)

        def norm_tiles(stack, name):
            return {"mean": sb(stack, name + "_mean", [P, CB]), "var": sb(stack, name + "_var", [P, CB]),
                    "std": sb(stack, name + "_std", [P, CB]), "xc": sb(stack, name + "_xc", [P, CB, D]),
                    "sq": sb(stack, name + "_sq", [P, CB, D])}

        def norm_sems(name):
            return {k: sem(name + "_" + k) for k in ("chain", "centred", "squared", "summed", "rooted")}

        st = ExitStack()
        t = norm_tiles(st, "n0")
        h = sb(st, "h", [P, CB, D])
        ht = sb(st, "ht", [P, CW])
        h_out = sb(st, "h_out", [P, CB, D])
        w_t = sb(st, "w_t", [P, D])
        a_cols = sb(st, "a_cols", [P, 2])
        ps_ht = ps(st, "ps_ht", [P, 1024])
        ps_h = ps(st, "ps_h", [P, 1024])
        ps_e = ps(st, "ps_e", [P, 512])
        s = norm_sems("n0")
        s["in"] = None
        s_w = sem("w0_loaded")
        s_wt = sem("w0_transposed")
        s_wtc = sem("w0_transpose_copied")
        s_wa = sem("w0_times_a")
        s_wext = sem("w0_extended")
        s_h = sem("h_normed")
        s_tp = sem("h_transposed")
        s_htc = sem("h_transpose_copied")
        s_hw = sem("h_projected")
        s_hwc = sem("h_projection_copied")
        s_hfree = sem("h_out_stored")
        block = nc.Block()
        with block:
            @block.sync
            def _(sp):
                sp.dma_start(wext[:, 0:D], w0).then_inc(s_w, 16)
                sp.dma_start(a_cols[:, 0:1], a_src.rearrange("(p a) -> p a", a=1)).then_inc(s_w, 16)
                sp.dma_start(a_cols[:, 1:2], a_dst.rearrange("(p a) -> p a", a=1)).then_inc(s_w, 16)
                sp.dma_start(bias0_col[:], bias0.rearrange("(p a) -> p a", a=1)).then_inc(s_w, 16)
                sp.sem_inc(s_hfree, 16)
                table = h_table.rearrange("(b p) f -> p b f", p=P)
                with sp.Fori(0, NC) as i:
                    sp.wait_ge(s_hwc, i + 1)
                    sp.dma_start(table[:, bass.ds(i * CB, CB), :], h_out[:]).then_inc(s_hfree, 16)
                sp.wait_ge(s_hfree, 16 * (NC + 1))

            @block.vector
            def _(dve):
                dve.wait_ge(s_wt, 1)
                dve.tensor_copy(w_t[:], ps_h[:, 0:D]).then_inc(s_wtc, 1)
                dve.wait_ge(s_wa, 1)
                dve.tensor_copy(wext[:, D:D + 2], ps_e[:, 0:2]).then_inc(s_wext, 1)
                with dve.Fori(0, NC) as i:
                    norm_vector(dve, i, x_sb[:, bass.ds(i * CB, CB), :], t, s)
                    dve.scalar_tensor_tensor(h[:], t["xc"][:], 0.0,
                                             t["std"][:, :].unsqueeze(2).broadcast_to([P, CB, D]),
                                             ALU.max, ALU.mult).then_inc(s_h, 1)

            @block.scalar
            def _(act):
                with act.Fori(0, NC) as i:
                    norm_scalar(act, i, t, s)
                    act.wait_ge(s_tp, i + 1)
                    act.activation(ht[:], ps_ht[:, 0:CW], ACT.Copy).then_inc(s_htc, 1)
                    hold(act, s_hw, i + 1)
                    hold(act, s_hfree, (i + 1) * 16)
                    pair = ps_e[:, 0:2 * CB].rearrange("p (b k) -> p b k", k=2)
                    act.activation(es_tab[:, bass.ds(i * CB, CB)], pair[:, :, 0], ACT.Copy)
                    act.activation(ed_tab[:, bass.ds(i * CB, CB)], pair[:, :, 1], ACT.Copy)
                    act.activation(h_out[:, :, :].rearrange("p b f -> p (b f)"), ps_h[:, 0:CW],
                                   ACT.Copy).then_inc(s_hwc, 1)

            @block.tensor
            def _(pe):
                pe.wait_ge(s_w, 64)
                pe.transpose(ps_h[:, 0:D], wext[:, 0:D], ident).then_inc(s_wt, 1)
                pe.wait_ge(s_wtc, 1)
                pe.matmul(ps_e[:, 0:2], w_t[:], a_cols[:], start=True, stop=True).then_inc(s_wa, 1)
                pe.wait_ge(s_wext, 1)
                with pe.Fori(0, NC) as i:
                    pe.wait_ge(s_h, i + 1)
                    for j in range(CB):
                        tp = pe.transpose(ps_ht[:, j * P:(j + 1) * P], h[:, j, :], ident)
                    tp.then_inc(s_tp, 1)
                    pe.wait_ge(s_htc, i + 1)
                    for j in range(CB):
                        pe.matmul(ps_h[:, j * P:(j + 1) * P], ht[:, j * P:(j + 1) * P], wext[:, 0:D],
                                  start=True, stop=True)
                        mm = pe.matmul(ps_e[:, 2 * j:2 * j + 2], ht[:, j * P:(j + 1) * P], wext[:, D:D + 2],
                                       start=True, stop=True)
                    mm.then_inc(s_hw, 1)
        st.close()

        st = ExitStack()
        HT = 16
        es_c = sb(st, "es_c", [P, T])
        ed_c = sb(st, "ed_c", [P, T])
        rows = [ps(st, f"ps_rows{b}", [P, 4, P]) for b in range(8)]
        lk = ExitStack()
        tabs = [[sb(lk, f"tab{a}{k}", [P, NB], BF16) for k in range(3)] for a in range(2)]
        rest = sb(lk, "rest", [P, NB])
        lo_rows = [[sb(lk, f"lo_rows{q}{a}", [P, HT * P], BF16) for a in range(2)] for q in range(2)]
        onehot = [[sb(lk, f"onehot{q}{a}", [P, HT * P], BF16) for a in range(2)] for q in range(2)]
        picked = sb(lk, "picked", [P, 32, NB])
        s_tab = sem("table_chain")
        s_lor = [sem(f"low_rows_loaded{q}") for q in range(2)]
        s_oh = sem("onehots_ready")
        s_pk = [sem(f"rows_picked{b}") for b in range(8)]
        s_sel = [sem(f"columns_picked{b}") for b in range(8)]
        block = nc.Block()
        with block:
            @block.sync
            def _(sp):
                with sp.Fori(0, T // HT // 2) as i:
                    for q in range(2):
                        hold(sp, s_oh, i * 2 + q + 1)
                        for a, flat in enumerate((lo_src_flat, lo_dst_flat)):
                            sp.dma_start(lo_rows[q][a][:],
                                         flat[bass.ds((i * 2 + q) * HT * P, HT * P)].partition_broadcast(P)
                                         ).then_inc(s_lor[q], 16)

            @block.vector
            def _(dve):
                link = Chain(dve, "split_chain")
                for a, tab in enumerate((es_tab, ed_tab)):
                    link(dve.tensor_copy(tabs[a][0][:], tab[:]))
                    link(dve.tensor_tensor(rest[:], tab[:], tabs[a][0][:], ALU.subtract))
                    link(dve.tensor_copy(tabs[a][1][:], rest[:]))
                    link(dve.tensor_tensor(rest[:], rest[:], tabs[a][1][:], ALU.subtract))
                    link(dve.tensor_copy(tabs[a][2][:], rest[:]))
                dve.sem_inc(s_oh, 2)
                with dve.Fori(0, T // HT // 2) as i:
                    for q in range(2):
                        hold(dve, s_lor[q], (i + 1) * 32)
                        dve.tensor_scalar(onehot[q][0][:], lo_rows[q][0][:], con[:, C_PART:C_PART + 1], None,
                                          ALU.is_equal)
                        dve.tensor_scalar(onehot[q][1][:], lo_rows[q][1][:], con[:, C_PART:C_PART + 1], None,
                                          ALU.is_equal).then_inc(s_oh, 1)
                        for b in range(8):
                            hold(dve, s_pk[b], i * 2 + q + 1)
                            hi, to = ((hi_src, es_c), (hi_dst, ed_c))[b // 4]
                            for j in range(4):
                                col = (i * 2 + q) * HT + (b % 4) * 4 + j
                                sel = dve.scalar_tensor_tensor(
                                    picked[:, b * 4 + j, :], iota[:, 0:NB], hi[:, bass.ds(col, 1)], rows[b][:, j, 0:NB],
                                    ALU.is_equal, ALU.mult, accum_out=to[:, bass.ds(col, 1)])
                            sel.then_inc(s_sel[b], 1)

            @block.tensor
            def _(pe):
                for b in range(8):
                    pe.sem_inc(s_sel[b], 1)
                with pe.Fori(0, T // HT // 2) as i:
                    for q in range(2):
                        hold(pe, s_oh, i * 2 + q + 3)
                        for b in range(8):
                            hold(pe, s_sel[b], i * 2 + q + 1)
                            for j in range(4):
                                tile = (b % 4) * 4 + j
                                for k in range(3):
                                    mm = pe.matmul(rows[b][:, j, 0:NB],
                                                   onehot[q][b // 4][:, tile * P:(tile + 1) * P],
                                                   tabs[b // 4][k][:], start=(k == 0), stop=(k == 2))
                            mm.then_inc(s_pk[b], 1)
        lk.close()

        sm = ExitStack()
        rows_e = sb(sm, "rows_e", [P, 13, P])
        long = {k: sb(sm, "long_" + k, [P, T]) for k in ("dst", "es", "ed", "same", "next", "a", "b", "m")}
        ends = sb(sm, "ends", [P, 4])
        carry = sb(sm, "carry", [P, 2])
        line = {k: sb(sm, "line_" + k, [1, P]) for k in
                ("head", "tail", "hv", "tv", "cont", "whole", "d0", "d1", "cin", "cout", "pc", "pw")}
        ramp_i = sb(sm, "ramp_i", [P, T], I32)
        ramp = sb(sm, "ramp", [P, T])
        s_erows = sem("edge_rows_transposed")
        s_erc = sem("edge_rows_copied")
        s_est = sem("edge_rows_stored")
        s_long = sem("long_rows_loaded")
        s_ramp = sem("ramp_ready")
        s_ends = sem("row_ends_ready")
        s_endt = sem("row_ends_transposed")
        s_car = sem("carries_ready")
        s_cart = sem("carries_transposed")
        s_diff = sem("scores_shifted")
        s_exp = sem("scores_exponentiated")
        s_al = sem("alpha_ready")
        s_als = sem("alpha_stored")
        s_alr = sem("alpha_rows_loaded")
        s_alt = sem("alpha_rows_transposed")
        back = rows
        block = nc.Block()
        with block:
            def piece(k):
                return back[k // 4][:, :, :].rearrange("p a b -> p (a b)")[:, (k % 4) * P:(k % 4 + 1) * P]

            line_ps = back[4][:, :, :].rearrange("p a b -> p (a b)")
            car_ps = back[5][:, :, :].rearrange("p a b -> p (a b)")

            @block.sync
            def _(sp):
                sp.dma_start(long["dst"][:].bitcast(I32), dst_flat.rearrange("(p m) -> p m", p=P)).then_inc(s_long, 16)
                for n, flat in enumerate((es_flat, ed_flat)):
                    sp.wait_ge(s_erc, n + 1)
                    sp.dma_start(flat[0:12 * P * P].rearrange("(k r e) -> r k e", k=12, r=P),
                                 rows_e[:, 0:12, :]).then_inc(s_est, 16)
                    sp.dma_start(flat[12 * P * P:EP].rearrange("(r e) -> r e", r=TR),
                                 rows_e[0:TR, 12, :]).then_inc(s_est, 16)
                    sp.wait_ge(s_est, 32 * (n + 1))
                    sp.dma_start(long[("es", "ed")[n]][:], flat.rearrange("(p m) -> p m", p=P)).then_inc(s_long, 16)
                sp.wait_ge(s_al, 1)
                sp.dma_start(alpha_flat.rearrange("(p m) -> p m", p=P), long["b"][:]).then_inc(s_als, 16)
                sp.wait_ge(s_als, 16)
                load_rows(sp, rows_e, alpha_flat, s_alr)

            @block.gpsimd
            def _(pool):
                pool.iota(ramp_i[:], pattern=[[1, T]], base=0, channel_multiplier=T).then_inc(s_ramp, 1)

            @block.tensor
            def _(pe):
                for n, columns in enumerate((es_c, ed_c)):
                    if n:
                        pe.wait_ge(s_erc, 1)
                    for k, r in PIECES:
                        tp = pe.transpose(piece(k)[0:r, :], columns[:, k * P:k * P + r], ident)
                    tp.then_inc(s_erows, 1)
                for n in range(2):
                    pe.wait_ge(s_ends, n + 1)
                    for k in range(4):
                        tp = pe.transpose(line_ps[0:1, k * P:(k + 1) * P], ends[:, k:k + 1], ident)
                    tp.then_inc(s_endt, 1)
                    pe.wait_ge(s_car, n + 1)
                    pe.transpose(car_ps[:, 0:1], line["cin"][:], ident[0:1, 0:1])
                    pe.transpose(car_ps[:, 1:2], line["cout"][:], ident[0:1, 0:1]).then_inc(s_cart, 1)
                pe.wait_ge(s_alr, 32)
                for k, r in PIECES:
                    tp = pe.transpose(piece(k)[:, 0:r], rows_e[0:r, k, :], ident[0:r, 0:r])
                tp.then_inc(s_alt, 1)

            @block.scalar
            def _(act):
                act.wait_ge(s_diff, 1)
                act.activation(long["a"][:], long["a"][:], ACT.Exp).then_inc(s_exp, 1)

            @block.vector
            def _(dve):
                link = Chain(dve, "softmax_chain")
                rev = slice(None, None, -1)
                dstl, same, nxt, a, b, m = (long[k] for k in ("dst", "same", "next", "a", "b", "m"))

                def copy_rows(n):
                    dve.wait_ge(s_erows, n + 1)
                    if n:
                        dve.wait_ge(s_est, 32 * n)
                    for k in range(4):
                        w = min(4, 13 - 4 * k)
                        r = TR if k == 3 else P
                        cp = dve.tensor_copy(rows_e[0:r, 4 * k:4 * k + w, :], back[k][0:r, 0:w, :])
                    cp.then_inc(s_erc, 1)

                copy_rows(0)
                copy_rows(1)
                dve.wait_ge(s_ramp, 1)
                dve.tensor_copy(ramp[:], ramp_i[:])
                dve.wait_ge(s_long, 48)
                link(dve.tensor_copy(m[:], dstl[:].bitcast(I32)))
                link(dve.tensor_copy(dstl[:], m[:]))
                link(dve.memset(same[:, 0:1], 0.0))
                link(dve.memset(nxt[:, T - 1:T], 0.0))
                dve.tensor_tensor(same[:, 1:T], dstl[:, 1:T], dstl[:, 0:T - 1], ALU.is_equal)
                link(dve.tensor_tensor(nxt[:, 0:T - 1], dstl[:, 1:T], dstl[:, 0:T - 1], ALU.is_equal))
                link(dve.tensor_scalar(b[:], same[:], 1.0, BIG, ALU.subtract, ALU.mult))
                link(dve.tensor_tensor_scan(a[:], b[:], long["es"][:], -BIG, ALU.add, ALU.max))
                link(dve.tensor_scalar(b[:], nxt[:], 1.0, BIG, ALU.subtract, ALU.mult))
                link(dve.tensor_tensor_scan(m[:, rev], b[:, rev], a[:, rev], -BIG, ALU.add, ALU.max))

                def row_ends(n, head_value, tail_value):
                    dve.tensor_copy(ends[:, 0:1], dstl[:, 0:1])
                    dve.tensor_copy(ends[:, 1:2], dstl[:, T - 1:T])
                    dve.tensor_copy(ends[:, 2:3], head_value)
                    dve.tensor_copy(ends[:, 3:4], tail_value).then_inc(s_ends, 1)
                    dve.wait_ge(s_endt, n + 1)
                    for k, name in enumerate(("head", "tail", "hv", "tv")):
                        link(dve.tensor_copy(line[name][:], line_ps[0:1, k * P:(k + 1) * P]))
                    link(dve.memset(line["cont"][:], 0.0))
                    link(dve.tensor_tensor(line["cont"][:, 1:P], line["head"][:, 1:P], line["tail"][:, 0:P - 1],
                                           ALU.is_equal))
                    link(dve.tensor_tensor(line["whole"][:], line["head"][:], line["tail"][:], ALU.is_equal))

                L = line
                row_ends(0, m[:, 0:1], a[:, T - 1:T])
                link(dve.tensor_scalar(L["pc"][:], L["cont"][:], 1.0, BIG, ALU.subtract, ALU.mult))
                link(dve.tensor_scalar(L["pw"][:], L["whole"][:], 1.0, BIG, ALU.subtract, ALU.mult))
                link(dve.memset(L["d0"][:], -BIG))
                link(dve.memset(L["d1"][:], -BIG))
                link(dve.tensor_tensor(L["d0"][:, 1:P], L["pw"][:, 0:P - 1], L["pc"][:, 1:P], ALU.add))
                link(dve.tensor_tensor(L["d1"][:, 1:P], L["tv"][:, 0:P - 1], L["pc"][:, 1:P], ALU.add))
                link(dve.tensor_tensor_scan(L["cin"][:], L["d0"][:], L["d1"][:], -BIG, ALU.add, ALU.max))
                link(dve.memset(L["d0"][:], -BIG))
                link(dve.memset(L["d1"][:], -BIG))
                link(dve.tensor_tensor(L["d0"][:, 0:P - 1], L["pw"][:, 1:P], L["pc"][:, 1:P], ALU.add))
                link(dve.tensor_tensor(L["d1"][:, 0:P - 1], L["hv"][:, 1:P], L["pc"][:, 1:P], ALU.add))
                link(dve.tensor_tensor_scan(L["cout"][:, rev], L["d0"][:, rev], L["d1"][:, rev], -BIG,
                                            ALU.add, ALU.max))
                dve.sem_inc(s_car, 1)
                dve.wait_ge(s_cart, 1)
                link(dve.tensor_copy(carry[:], car_ps[:, 0:2]))
                for k, end in enumerate((dstl[:, 0:1], dstl[:, T - 1:T])):
                    link(dve.tensor_scalar(b[:], dstl[:], end, -BIG, ALU.not_equal, ALU.mult))
                    link(dve.scalar_tensor_tensor(m[:], b[:], carry[:, k:k + 1], m[:], ALU.add, ALU.max))
                link(dve.tensor_tensor(a[:], long["es"][:], long["ed"][:], ALU.add))
                link(dve.scalar_tensor_tensor(a[:], a[:], SLOPE, a[:], ALU.mult, ALU.max))
                link(dve.tensor_tensor(m[:], m[:], long["ed"][:], ALU.add))
                link(dve.scalar_tensor_tensor(m[:], m[:], SLOPE, m[:], ALU.mult, ALU.max))
                dve.tensor_tensor(a[:], a[:], m[:], ALU.subtract).then_inc(s_diff, 1)
                dve.wait_ge(s_exp, 1)
                p_e = long["es"]
                link(dve.scalar_tensor_tensor(p_e[:], ramp[:], float(E), a[:], ALU.is_lt, ALU.mult))
                link(dve.tensor_tensor_scan(a[:], same[:], p_e[:], 0.0, ALU.mult, ALU.add))
                link(dve.scalar_tensor_tensor(b[:], nxt[:], 0.0, a[:], ALU.is_equal, ALU.mult))
                link(dve.tensor_tensor_scan(m[:, rev], nxt[:, rev], b[:, rev], 0.0, ALU.mult, ALU.add))
                row_ends(1, m[:, 0:1], a[:, T - 1:T])
                link(dve.memset(L["d0"][:], 0.0))
                link(dve.memset(L["d1"][:], 0.0))
                link(dve.tensor_tensor(L["d0"][:, 1:P], L["whole"][:, 0:P - 1], L["cont"][:, 1:P], ALU.mult))
                link(dve.tensor_tensor(L["d1"][:, 1:P], L["tv"][:, 0:P - 1], L["cont"][:, 1:P], ALU.mult))
                link(dve.tensor_tensor_scan(L["cin"][:], L["d0"][:], L["d1"][:], 0.0, ALU.mult, ALU.add))
                link(dve.memset(L["d0"][:], 0.0))
                link(dve.memset(L["d1"][:], 0.0))
                link(dve.tensor_tensor(L["d0"][:, 0:P - 1], L["whole"][:, 1:P], L["cont"][:, 1:P], ALU.mult))
                link(dve.tensor_tensor(L["d1"][:, 0:P - 1], L["hv"][:, 1:P], L["cont"][:, 1:P], ALU.mult))
                link(dve.tensor_tensor_scan(L["cout"][:, rev], L["d0"][:, rev], L["d1"][:, rev], 0.0,
                                            ALU.mult, ALU.add))
                dve.sem_inc(s_car, 1)
                dve.wait_ge(s_cart, 2)
                link(dve.tensor_copy(carry[:], car_ps[:, 0:2]))
                for k, end in enumerate((dstl[:, 0:1], dstl[:, T - 1:T])):
                    link(dve.tensor_scalar(b[:], dstl[:], end, carry[:, k:k + 1], ALU.is_equal, ALU.mult))
                    link(dve.tensor_tensor(m[:], m[:], b[:], ALU.add))
                link(dve.tensor_scalar(m[:], m[:], 1e-15, None, ALU.max))
                link(dve.reciprocal(m[:], m[:]))
                dve.tensor_tensor(b[:], p_e[:], m[:], ALU.mult).then_inc(s_al, 1)
                dve.wait_ge(s_alt, 1)
                for k in range(4):
                    w = min(512, T - 512 * k)
                    cp = dve.tensor_copy(alpha[:, 512 * k:512 * k + w],
                                         back[k][:, :, :].rearrange("p a b -> p (a b)")[:, 0:w])
                link(cp)
        sm.close()
        st.close()

        agg_stack = ExitStack()
        agg = sb(agg_stack, "agg", [P, AW])
        st = ExitStack()
        stage = [sb(st, f"stage{q}", [P, GT], I32) for q in range(2)]
        gath = sb(st, "gath", [P, 2 * GT, D])
        spread = sb(st, "spread", [P, 2 * GT, W])
        dl_now = sb(st, "dl_now", [P, T])
        base_now = sb(st, "base_now", [1, NG], I32)
        ps_w = [ps(st, f"ps_w{q}", [P, 512]) for q in range(2)]
        s_aggz = sem("agg_zeroed")
        s_stage = sem("indices_staged")
        s_gath = [sem(f"rows_gathered{k}") for k in range(2 * GT)]
        s_spread = sem("spread_ready")
        s_win = sem("window_summed")
        s_added = sem("window_added")
        s_shift = sem("window_shifted")
        block = nc.Block()
        with block:
            def pass_count(eng):
                return eng.value_load(passes[0:1, 0:1], min_val=1, max_val=NB + 1)

            @block.scalar
            def _(act):
                n_pass = pass_count(act)
                with act.Fori(0, n_pass) as k:
                    with act.Fori(0, NG // 2) as i:
                        for q in range(2):
                            g = k * NG + i * 2 + q
                            hold(act, s_win, g + 1)
                            act.activation(stage[q][:], src_i[:, bass.ds((i * 2 + q) * GT, GT)],
                                           ACT.Copy).then_inc(s_stage, 1)

            @block.gpsimd
            def _(pool):
                n_pass = pass_count(pool)
                with pool.Fori(0, n_pass) as k:
                    with pool.Fori(0, NG // 2) as i:
                        for q in range(2):
                            hold(pool, s_stage, k * NG + i * 2 + q + 1)
                            for j in range(GT):
                                pool.indirect_dma_start(
                                    gath[:, q * GT + j, :], None, h_table,
                                    bass.IndirectOffsetOnAxis(ap=stage[q][:, j:j + 1], axis=0)
                                ).then_inc(s_gath[q * GT + j], 16)

            @block.vector
            def _(dve):
                dve.memset(agg[:], 0.0).then_inc(s_added, 1)
                dve.tensor_copy(dl_now[:], dl[:])
                dve.tensor_copy(base_now[:], base_i[:]).then_inc(s_shift, 1)
                dve.wait_ge(s_shift, 1)
                n_pass = pass_count(dve)
                with dve.Fori(0, n_pass) as k:
                    with dve.Fori(0, NG // 2) as i:
                        for q in range(2):
                            g = k * NG + i * 2 + q
                            hold(dve, s_win, g + 1)
                            for j in range(GT):
                                col = (i * 2 + q) * GT + j
                                sp_ = dve.tensor_scalar(spread[:, q * GT + j, :], iota,
                                                        dl_now[:, bass.ds(col, 1)], alpha[:, bass.ds(col, 1)],
                                                        ALU.is_equal, ALU.mult)
                            sp_.then_inc(s_spread, 1)
                            base = dve.value_load(base_now[0:1, bass.ds(i * 2 + q, 1)], min_val=0, max_val=NP)
                            hold(dve, s_win, g + 3)
                            hold(dve, s_added, g + 1)
                            dve.tensor_tensor(agg[:, bass.ds(base, W)], agg[:, bass.ds(base, W)],
                                              ps_w[q][:, 0:W], ALU.add).then_inc(s_added, 1)
                    dve.tensor_scalar(base_now[:], base_now[:], float(W), float(NP), ALU.add, ALU.min)
                    dve.tensor_scalar(dl_now[:], dl_now[:], -float(W), None, ALU.add).then_inc(s_shift, 1)
                    hold(dve, s_shift, k + 2)

            @block.tensor
            def _(pe):
                pe.sem_inc(s_win, 2)
                n_pass = pass_count(pe)
                with pe.Fori(0, n_pass) as k:
                    with pe.Fori(0, NG // 2) as i:
                        for q in range(2):
                            g = k * NG + i * 2 + q
                            hold(pe, s_spread, g + 1)
                            for j in range(GT):
                                hold(pe, s_gath[q * GT + j], (k * (NG // 2) + i + 1) * 16)
                                mm = pe.matmul(ps_w[q][:, 0:W], gath[:, q * GT + j, :],
                                               spread[:, q * GT + j, :], start=(j == 0), stop=(j == GT - 1))
                            mm.then_inc(s_win, 1)
        st.close()

        st = ExitStack()
        t = norm_tiles(st, "n1")
        below = sb(st, "below", [P, CW])
        above = sb(st, "above", [P, CW])
        elu = sb(st, "elu", [P, CW])
        h2_out = sb(st, "h2_out", [P, CB, D])
        ps_x = ps(st, "ps_x", [P, 1024])
        s = norm_sems("n1")
        s_neg = sem("negative_part_ready")
        s_nexp = sem("negative_part_exponentiated")
        s_elu = sem("elu_ready")
        s_elut = sem("elu_transposed")
        s_in1 = sem("residual_added")
        s_h2 = sem("h2_normed")
        s_h2s = sem("h2_stored")
        s["in"] = s_in1
        block = nc.Block()
        with block:
            @block.vector
            def _(dve):
                with dve.Fori(0, NC) as i:
                    part = agg[:, bass.ds(i * CW, CW)]
                    dve.tensor_scalar(above[:], part, bias0_col[:], 0.0, ALU.add, ALU.max)
                    dve.tensor_scalar(below[:], part, bias0_col[:], 0.0, ALU.add, ALU.min).then_inc(s_neg, 1)
                    hold(dve, s_nexp, i + 1)
                    dve.scalar_tensor_tensor(elu[:], below[:], -1.0, above[:], ALU.add, ALU.add).then_inc(s_elu, 1)
                    here = x_sb[:, bass.ds(i * CB, CB), :]
                    hold(dve, s_elut, i + 1)
                    dve.tensor_tensor(here, here, ps_x[:, 0:CW].rearrange("p (b f) -> p b f", f=D),
                                      ALU.add).then_inc(s_in1, 1)
                    norm_vector(dve, i, here, t, s)
                    hold(dve, s_h2s, (i + 1) * 16)
                    dve.scalar_tensor_tensor(h2_out[:], t["xc"][:], 0.0,
                                             t["std"][:, :].unsqueeze(2).broadcast_to([P, CB, D]),
                                             ALU.max, ALU.mult).then_inc(s_h2, 1)

            @block.scalar
            def _(act):
                with act.Fori(0, NC) as i:
                    hold(act, s_neg, i + 1)
                    act.activation(below[:], below[:], ACT.Exp).then_inc(s_nexp, 1)
                    norm_scalar(act, i, t, s)

            @block.tensor
            def _(pe):
                with pe.Fori(0, NC) as i:
                    hold(pe, s_elu, i + 1)
                    for j in range(CB):
                        tp = pe.transpose(ps_x[:, j * P:(j + 1) * P], elu[:, j * P:(j + 1) * P], ident)
                    tp.then_inc(s_elut, 1)

            @block.sync
            def _(sp):
                table = h2_table[0:NP, :].rearrange("(b p) f -> p b f", p=P)
                sp.sem_inc(s_h2s, 16)
                with sp.Fori(0, NC) as i:
                    sp.wait_ge(s_h2, i + 1)
                    sp.dma_start(table[:, bass.ds(i * CB, CB), :], h2_out[:]).then_inc(s_h2s, 16)
                sp.wait_ge(s_h2s, 16 * (NC + 1))
        st.close()
        agg_stack.close()
        to_layer1.close()

        st = ExitStack()
        HG = GT // 2
        w_c = sb(st, "w_c", [P, T])
        dl_now = sb(st, "dl_now1", [P, T])
        base_now = sb(st, "base_now1", [1, NG], I32)
        win = [sb(st, f"win{q}", [P, D]) for q in range(2)]
        srow = [sb(st, f"srow{q}", [P, GT * P], I16) for q in range(2)]
        equal = sb(st, "equal", [P, 2 * GT, P])
        place = sb(st, "place", [P, 2 * GT, W])
        mix = sb(st, "mix", [P, 2 * GT, P])
        val = sb(st, "val", [P, 2 * GT, RW])
        idx = [sb(st, f"idx{q}", [P, GT], I32) for q in range(2)]
        dup = sb(st, "dup", [P, 3, GT])
        ps_mix = [ps(st, f"ps_mix{h}", [P, HG, P]) for h in range(2)]
        ps_val = [ps(st, f"ps_val{h}", [P, HG, D]) for h in range(2)]
        ps_sum = [ps(st, f"ps_sum{q}", [P, GT, 4]) for q in range(2)]
        s_start = sem("layer1_started")
        s_srow = [sem(f"sources_loaded{q}") for q in range(2)]
        s_win1 = [sem(f"window_loaded{q}") for q in range(2)]
        s_built = sem("masks_built")
        s_sum = sem("source_sums_ready")
        s_mixp = [sem(f"mix_product{h}") for h in range(2)]
        s_mixc = [sem(f"mix_copied{h}") for h in range(2)]
        s_valp = [sem(f"value_product{h}") for h in range(2)]
        s_valc = [sem(f"value_copied{h}") for h in range(2)]
        s_dup = sem("index_chain")
        s_idx = sem("indices_ready")
        s_scat = [sem(f"scattered{k}") for k in range(NACC)]
        s_reuse = sem("half_reusable")
        s_trash = sem("trash_rows_ready")
        trash_i = sb(st, "trash_i", [P, 1], I32)
        nothing = sb(st, "nothing", [P, RW])
        block = nc.Block()
        with block:
            def buffers_scattered(eng, g):
                hold(eng, s_reuse, g + 1)

            @block.sync
            def _(sp):
                n_pass = pass_count(sp)
                with sp.Fori(0, n_pass) as k:
                    hold(sp, s_start, k + 1)
                    with sp.Fori(0, NG // 2) as i:
                        for q in range(2):
                            g = k * NG + i * 2 + q
                            base = sp.value_load(base_now[0:1, bass.ds(i * 2 + q, 1)], min_val=0, max_val=NP)
                            hold(sp, s_valp[1], g + 1)
                            sp.dma_start(srow[q][:], src16_flat[bass.ds((i * 2 + q) * GT * P, GT * P)
                                                                ].partition_broadcast(P)).then_inc(s_srow[q], 16)
                            sp.dma_start(win[q][:], h2_table[bass.ds(base, W), :]).then_inc(s_win1[q], 16)

            @block.vector
            def _(dve):
                dve.tensor_copy(w_c[:], r4[:, :, 0])
                dve.tensor_copy(dl_now[:], dl[:])
                dve.memset(nothing[:], 0.0)
                dve.tensor_copy(trash_i[:], con[:, C_TRASH:C_TRASH + 1]).then_inc(s_trash, 1)
                dve.tensor_copy(base_now[:], base_i[:]).then_inc(s_start, 1)
                dve.wait_ge(s_start, 1)
                n_pass = pass_count(dve)
                with dve.Fori(0, n_pass) as k:
                    with dve.Fori(0, NG // 2) as i:
                        for q in range(2):
                            g = k * NG + i * 2 + q
                            hold(dve, s_srow[q], (k * (NG // 2) + i + 1) * 16)
                            for j in range(GT):
                                col = (i * 2 + q) * GT + j
                                slot = q * GT + j
                                dve.tensor_scalar(equal[:, slot, :], srow[q][:, j * P:(j + 1) * P],
                                                  src_c[:, bass.ds(col, 1)], None, ALU.is_equal)
                                bt = dve.tensor_scalar(place[:, slot, :], iota, dl_now[:, bass.ds(col, 1)],
                                                       w_c[:, bass.ds(col, 1)], ALU.is_equal, ALU.mult)
                            bt.then_inc(s_built, 1)
                            hold(dve, s_sum, g + 1)
                            sums = ps_sum[q]
                            own = src_c[:, bass.ds((i * 2 + q) * GT, GT)]
                            dve.tensor_scalar(dup[:, 0, :], sums[:, :, 2], con[:, C_T0:C_T0 + 1], None,
                                              ALU.is_ge).then_inc(s_dup, 1)
                            hold(dve, s_dup, g * 3 + 1)
                            dve.scalar_tensor_tensor(dup[:, 1, :], sums[:, :, 3], con[:, C_T1:C_T1 + 1],
                                                     dup[:, 0, :], ALU.is_ge, ALU.max).then_inc(s_dup, 1)
                            hold(dve, s_dup, g * 3 + 2)
                            dve.scalar_tensor_tensor(dup[:, 2, :], own, con[:, C_TRASH:C_TRASH + 1],
                                                     dup[:, 1, :], ALU.subtract, ALU.mult).then_inc(s_dup, 1)
                            buffers_scattered(dve, g)
                            hold(dve, s_dup, g * 3 + 3)
                            dve.tensor_copy(val[:, q * GT:(q + 1) * GT, D:RW], sums[:, :, 0:2])
                            dve.tensor_tensor(idx[q][:], own, dup[:, 2, :], ALU.subtract).then_inc(s_idx, 1)
                    dve.memset(r4[:, :, 0:2], 0.0)
                    dve.tensor_scalar(base_now[:], base_now[:], float(W), float(NP), ALU.add, ALU.min)
                    dve.tensor_scalar(dl_now[:], dl_now[:], -float(W), None, ALU.add).then_inc(s_start, 1)
                    hold(dve, s_start, k + 2)

            @block.tensor
            def _(pe):
                pe.sem_inc(s_valp[1], 2)
                n_pass = pass_count(pe)
                with pe.Fori(0, n_pass) as k:
                    with pe.Fori(0, NG // 2) as i:
                        for q in range(2):
                            g = k * NG + i * 2 + q
                            hold(pe, s_built, g + 1)
                            for j in range(GT):
                                mm = pe.matmul(ps_sum[q][:, j, :], equal[:, q * GT + j, :],
                                               r4[:, bass.ds((i * 2 + q) * GT + j, 1), :].rearrange(
                                                   "p a c -> p (a c)"), start=True, stop=True)
                            mm.then_inc(s_sum, 1)
                            for h in range(2):
                                for j in range(HG):
                                    slot = q * GT + h * HG + j
                                    mm = pe.matmul(ps_mix[h][:, j, :], place[:, slot, :], equal[:, slot, :],
                                                   start=True, stop=True)
                                mm.then_inc(s_mixp[h], 1)
                            hold(pe, s_win1[q], (k * (NG // 2) + i + 1) * 16)
                            for h in range(2):
                                hold(pe, s_mixc[h], g + 1)
                                hold(pe, s_valc[h], g + 1)
                                for j in range(HG):
                                    mm = pe.matmul(ps_val[h][:, j, :], mix[:, q * GT + h * HG + j, :], win[q][:],
                                                   start=True, stop=True)
                                mm.then_inc(s_valp[h], 1)

            @block.scalar
            def _(act):
                act.sem_inc(s_valc[0], 1)
                act.sem_inc(s_valc[1], 1)
                n_pass = pass_count(act)
                with act.Fori(0, n_pass) as k:
                    with act.Fori(0, NG // 2) as i:
                        for q in range(2):
                            g = k * NG + i * 2 + q
                            for h in range(2):
                                hold(act, s_mixp[h], g + 1)
                                lo = q * GT + h * HG
                                act.activation(mix[:, lo:lo + HG, :], ps_mix[h][:, :, :],
                                               ACT.Copy).then_inc(s_mixc[h], 1)
                            buffers_scattered(act, g)
                            for h in range(2):
                                hold(act, s_valp[h], g + (1 if h == 0 else 3))
                                lo = q * GT + h * HG
                                act.activation(val[:, lo:lo + HG, 0:D], ps_val[h][:, :, :],
                                               ACT.Copy).then_inc(s_valc[h], 1)

            @block.gpsimd
            def _(pool):
                pool.wait_ge(s_trash, 1)
                for a in range(NACC):
                    pool.indirect_dma_start(
                        acc[a], bass.IndirectOffsetOnAxis(ap=trash_i[:, 0:1], axis=0), nothing[:], None,
                        compute_op=ALU.add).then_inc(s_scat[a], 16)
                pool.sem_inc(s_reuse, 1)
                n_pass = pass_count(pool)
                with pool.Fori(0, n_pass) as k:
                    with pool.Fori(0, NG // 2) as i:
                        for q in range(2):
                            g = k * NG + i * 2 + q
                            hold(pool, s_idx, g + 1)
                            for j in range(GT):
                                if j % HG == 0:
                                    hold(pool, s_valc[j // HG], g + 2)
                                hold(pool, s_scat[j % NACC], g * 32 + 16 + 16 * (j // NACC))
                                pool.indirect_dma_start(
                                    acc[j % NACC], bass.IndirectOffsetOnAxis(ap=idx[q][:, j:j + 1], axis=0),
                                    val[:, q * GT + j, :], None, compute_op=ALU.add
                                ).then_inc(s_scat[j % NACC], 16)
                                if j == NACC - 1:
                                    pool.sem_inc(s_reuse, 1)
                for a in range(NACC):
                    hold(pool, s_scat[a], n_pass * (NG * 32) + 16)
        st.close()

        st = ExitStack()
        w_top = sb(st, "w_top", [P, D])
        w_bot = sb(st, "w_bot", [P, D])
        bias1_row = sb(st, "bias1_row", [P, D])
        part_acc = sb(st, "part_acc", [P, NACC, CB, RW])
        h2_in = sb(st, "h2_in", [P, CB, D])
        two = sb(st, "two", [P, CB, 2, D])
        two_t = sb(st, "two_t", [P, CB, 2, P])
        cnt = sb(st, "cnt", [P, CB])
        rec = sb(st, "rec", [P, CB])
        wsum = sb(st, "wsum", [P, CB])
        ps_tt = ps(st, "ps_tt", [P, 2048])
        ps_o = ps(st, "ps_o", [P, 1024])
        s_w1 = sem("w1_loaded")
        s_part = sem("sums_loaded")
        s_pfree = sem("sums_used")
        s_fin = sem("final_chain")
        s_two = sem("mean_rows_ready")
        s_twot = sem("mean_rows_transposed")
        s_twoc = sem("mean_columns_copied")
        s_proj = sem("mean_projected")
        s_res = sem("result_ready")
        s_out = sem("result_stored")
        block = nc.Block()
        with block:
            @block.sync
            def _(sp):
                sp.dma_start(w_top[:], w1[0:D, :]).then_inc(s_w1, 16)
                sp.dma_start(w_bot[:], w1[D:2 * D, :]).then_inc(s_w1, 16)
                sp.dma_start(bias1_row[:], bias1.partition_broadcast(P)).then_inc(s_w1, 16)
                views = [a[0:NP, :].rearrange("(b p) c -> p b c", p=P) for a in acc]
                table = h2_table[0:NP, :].rearrange("(b p) f -> p b f", p=P)
                sp.sem_inc(s_pfree, 1)
                with sp.Fori(0, NC) as i:
                    hold(sp, s_pfree, i + 1)
                    for a in range(NACC):
                        sp.dma_start(part_acc[:, a, :, :], views[a][:, bass.ds(i * CB, CB), :]).then_inc(s_part, 16)
                    sp.dma_start(h2_in[:], table[:, bass.ds(i * CB, CB), :]).then_inc(s_part, 16)

            @block.vector
            def _(dve):
                dve.wait_ge(s_w1, 48)
                with dve.Fori(0, NC) as i:
                    def link(instruction, n):
                        instruction.then_inc(s_fin, 1)
                        hold(dve, s_fin, i * 7 + n)

                    hold(dve, s_part, (i + 1) * 80)
                    flat = part_acc[:, :, :, :].rearrange("p a b c -> p a (b c)")
                    link(dve.tensor_tensor(flat[:, 0:2, :], flat[:, 0:2, :], flat[:, 2:4, :], ALU.add), 1)
                    link(dve.tensor_tensor(flat[:, 0, :], flat[:, 0, :], flat[:, 1, :], ALU.add), 2)
                    link(dve.tensor_scalar(cnt[:], part_acc[:, 0, :, D + 1], 1.0, None, ALU.max), 3)
                    link(dve.reciprocal(rec[:], cnt[:]), 4)
                    link(dve.tensor_tensor(wsum[:], part_acc[:, 0, :, D], rec[:], ALU.mult), 5)
                    dve.tensor_tensor(two[:, :, 0, :], h2_in[:], wsum[:, :].unsqueeze(2).broadcast_to([P, CB, D]),
                                      ALU.mult)
                    dve.tensor_tensor(two[:, :, 1, :], part_acc[:, 0, :, 0:D],
                                      rec[:, :].unsqueeze(2).broadcast_to([P, CB, D]),
                                      ALU.mult).then_inc(s_two, 1)
                    here = x_sb[:, bass.ds(i * CB, CB), :]
                    link(dve.tensor_tensor(here, here, bias1_row[:, :].unsqueeze(1).broadcast_to([P, CB, D]),
                                           ALU.add), 6)
                    dve.sem_inc(s_pfree, 1)
                    hold(dve, s_proj, i + 1)
                    link(dve.tensor_tensor(here, here, ps_o[:, 0:CW].rearrange("p (b f) -> p b f", f=D),
                                           ALU.add), 7)
                    dve.sem_inc(s_res, 1)

            @block.tensor
            def _(pe):
                pe.wait_ge(s_w1, 48)
                with pe.Fori(0, NC) as i:
                    hold(pe, s_two, i + 1)
                    for b in range(2 * CB):
                        tp = pe.transpose(ps_tt[:, b * P:(b + 1) * P], two[:, b // 2, b % 2, :], ident)
                    tp.then_inc(s_twot, 1)
                    hold(pe, s_twoc, i + 1)
                    for b in range(CB):
                        pe.matmul(ps_o[:, b * P:(b + 1) * P], two_t[:, b, 0, :], w_top[:], start=True, stop=False)
                        mm = pe.matmul(ps_o[:, b * P:(b + 1) * P], two_t[:, b, 1, :], w_bot[:],
                                       start=False, stop=True)
                    mm.then_inc(s_proj, 1)

            @block.scalar
            def _(act):
                results = out[0:(NB - 1) * P, :].rearrange("(b p) f -> p b f", p=P)
                with act.Fori(0, NC) as i:
                    hold(act, s_twot, i + 1)
                    act.activation(two_t[:, :, :, :].rearrange("p b k f -> p (b k f)"), ps_tt[:, 0:2 * CW],
                                   ACT.Copy).then_inc(s_twoc, 1)
                with act.Fori(0, NC - 1) as i:
                    hold(act, s_res, i + 1)
                    act.dma_start(results[:, bass.ds(i * CB, CB), :],
                                  x_sb[:, bass.ds(i * CB, CB), :]).then_inc(s_out, 16)
                act.wait_ge(s_res, NC)
                act.dma_start(results[:, (NC - 1) * CB:NB - 1, :],
                              x_sb[:, (NC - 1) * CB:NB - 1, :]).then_inc(s_out, 16)
                act.dma_start(out[(NB - 1) * P:N, :], x_sb[0:N - (NB - 1) * P, NB - 1, :]).then_inc(s_out, 16)
                act.wait_ge(s_out, 16 * (NC + 1))
        st.close()


def kernel(x, src, dst, edge_weight1, L0_gnn_W, L0_gnn_a_src, L0_gnn_a_dst, L0_gnn_bias,
           L1_gnn_weight, L1_gnn_bias):
    import numpy as _np
    import concourse.bacc as _bacc
    from concourse.bass_utils import run_bass_kernel_spmd as _run

    nc = _bacc.Bacc("TRN2", target_bir_lowering=False, num_devices=1)
    arrays = {
        "x": _np.asarray(x), "src": _np.asarray(src), "dst": _np.asarray(dst),
        "weight": _np.asarray(edge_weight1).reshape(E), "w0": _np.asarray(L0_gnn_W),
        "a_src": _np.asarray(L0_gnn_a_src), "a_dst": _np.asarray(L0_gnn_a_dst),
        "bias0": _np.asarray(L0_gnn_bias), "w1": _np.asarray(L1_gnn_weight),
        "bias1": _np.asarray(L1_gnn_bias), "consts": shape_constants(),
    }
    args = [nc.dram_tensor(n, a.shape, mybir.dt.from_np(a.dtype), kind="ExternalInput").ap()
            for n, a in arrays.items()]
    out = nc.dram_tensor("out", (N, D), F32, kind="ExternalOutput").ap()
    build(nc, *args, out)
    got = _run(nc, [arrays], core_ids=[0])
    return got.results[0]["out"]
```

```python
from contextlib import ExitStack

import numpy as np

import concourse.bass as bass
from concourse import mybir

F32 = mybir.dt.float32
BF16 = mybir.dt.bfloat16
I32 = mybir.dt.int32
I16 = mybir.dt.int16
ALU = mybir.AluOpType
ACT = mybir.ActivationFunctionType
X = mybir.AxisListType.X

P = 128
N = 12500
E = 200000
D = 128
NB = -(-N // P)
NP = NB * P
W = 128
GT = 8
T = 1568
EP = T * P
NG = T // GT
TR = T - 12 * P
PIECES = [(k, P) for k in range(12)] + [(12, TR)]
CB = 7
NC = NB // CB
CT = 112
NCH = T // CT
CG = CT // GT
SOFTMAX_AT = (0, 1, 5, 6, 7)
QUESTION_AT = {0: 2, 1: 3, 6: 4, 7: 5, 8: 6}
EXPONENTIALS_AT = 3
CW = CB * P
AW = NP + W
NACC = 4
RW = D + 2
BIG = 1e30
EPS = 1e-5
SLOPE = 0.2

C_ID, C_IOTA, C_ROW0, C_PART, C_U0, C_U1, C_T0, C_T1, C_TRASH, C_EPS, C_TRI, C_ONES = (
    0, 128, 256, 384, 385, 386, 387, 388, 389, 390, 391, 519)
C_WIDTH = 647


def shape_constants():
    c = np.zeros((P, C_WIDTH), np.float32)
    p = np.arange(P)
    c[:, C_ID:C_ID + P] = np.eye(P)
    c[:, C_IOTA:C_IOTA + P] = p[None, :]
    c[0, C_ROW0:C_ROW0 + P] = 1.0
    c[:, C_PART] = p
    power = 4.0 ** (32 - p % 64)
    low = p < 64
    c[:, C_U0] = np.where(low, power, 0.0)
    c[:, C_U1] = np.where(low, 0.0, power)
    c[:, C_T0] = np.where(low, 2 * power, 4.0 ** -32)
    c[:, C_T1] = np.where(low, BIG, 2 * power)
    c[:, C_TRASH] = NP + p
    c[:, C_EPS] = EPS
    c[:, C_TRI:C_TRI + P] = (p[:, None] < p[None, :])
    c[:, C_ONES:C_ONES + P] = 1.0
    return c


def build(nc, x, src, dst, weight, w0, a_src, a_dst, bias0, w1, bias1, consts, out):
    def dram(name, shape, dt):
        return nc.dram_tensor(name, shape, dt, kind="Internal").ap()

    src_flat = dram("src_flat", (EP,), I32)
    dst_flat = dram("dst_flat", (EP,), I32)
    wgt_flat = dram("wgt_flat", (EP,), F32)
    lo_src_flat = dram("lo_src_flat", (EP,), BF16)
    lo_dst_flat = dram("lo_dst_flat", (EP,), BF16)
    src16_flat = dram("src16_flat", (EP,), I16)
    h_table = dram("h_table", (NP, D), F32)
    h2_table = dram("h2_table", (AW, D), F32)
    acc = [dram(f"acc{k}", (AW, RW), F32) for k in range(NACC)]

    whole = ExitStack()

    def sb(stack, name, shape, dt=F32):
        return stack.enter_context(nc.sbuf_tensor(name, shape, dt))

    def ps(stack, name, shape, dt=F32):
        return stack.enter_context(nc.psum_tensor(name, shape, dt))

    def sem(name):
        return whole.enter_context(nc.semaphore(name))

    passed = sem("passed")

    def hold(eng, semaphore, value):
        eng.wait_ge(semaphore, value)
        eng.sem_inc(passed, 1)

    class Chain:

        def __init__(self, eng, name):
            self.eng, self.sem, self.n = eng, sem(name), 0

        def __call__(self, instruction):
            self.n += 1
            instruction.then_inc(self.sem, 1)
            self.eng.wait_ge(self.sem, self.n)

    with whole:
        con = sb(whole, "con", [P, C_WIDTH])
        ident = con[:, C_ID:C_ID + P]
        iota = con[:, C_IOTA:C_IOTA + P]
        src_c = sb(whole, "src_c", [P, T])
        neg_dl = sb(whole, "neg_dl", [P, T])
        dl = sb(whole, "dl", [P, T])
        w_c = sb(whole, "w_c", [P, T])
        base_i = sb(whole, "base_i", [1, NG], I32)
        passes = sb(whole, "passes", [1, 1], I32)
        unsorted = sb(whole, "unsorted", [1, 1], I32)
        bias0_col = sb(whole, "bias0_col", [P, 1])

        to_layer1 = ExitStack()
        src_i = sb(to_layer1, "src_i", [P, T], I32)
        wext = sb(to_layer1, "wext", [P, D + 2])
        es_tab = sb(to_layer1, "es_tab", [P, NB])
        ed_tab = sb(to_layer1, "ed_tab", [P, NB])
        hi_src = sb(to_layer1, "hi_src", [P, T])
        hi_dst = sb(to_layer1, "hi_dst", [P, T])

        xs = ExitStack()
        x_sb = sb(xs, "x_sb", [P, NB, D])

        s_copied = sem("edges_copied")
        s_con = sem("constants_loaded")
        s_x = sem("x_loaded")
        s_xz = sem("x_padding_zeroed")
        s_zero = sem("zeros_written")
        s_zt = sem("zero_tile")
        zs = ExitStack()
        no_weight = sb(zs, "no_weight", [1, EP - E])
        block = nc.Block()
        with block:
            @block.sync
            def _(sp):
                sp.dma_start(con[:], consts).then_inc(s_con, 16)
                for a, b in ((src_flat, src), (dst_flat, dst), (wgt_flat, weight)):
                    sp.dma_start(a[0:E].rearrange("(a b) -> a b", a=P // 2),
                                 b[0:E].rearrange("(a b) -> a b", a=P // 2)).then_inc(s_copied, 16)
                for a, b in ((src_flat, src), (dst_flat, dst)):
                    sp.dma_start(a[E:EP].rearrange("(a b) -> a b", b=1),
                                 b[E - 1:E].partition_broadcast(EP - E)).then_inc(s_copied, 16)
                sp.wait_ge(s_zt, 1)
                sp.dma_start(wgt_flat[E:EP].rearrange("(a b) -> a b", a=1),
                             no_weight[:]).then_inc(s_copied, 16)
                sp.wait_ge(s_con, 16)
                sp.wait_ge(s_copied, 96)

            @block.scalar
            def _(act):
                act.wait_ge(s_xz, 1)
                act.dma_start(x_sb[:, 0:NB - 1, :],
                              x[0:(NB - 1) * P, :].rearrange("(b p) f -> p b f", p=P)).then_inc(s_x, 16)
                act.dma_start(x_sb[0:N - (NB - 1) * P, NB - 1, :], x[(NB - 1) * P:N, :]).then_inc(s_x, 16)

            @block.vector
            def _(dve):
                dve.memset(x_sb[:, NB - 1, :], 0.0).then_inc(s_xz, 1)
                dve.memset(no_weight[:], 0.0).then_inc(s_zt, 1)
        zs.close()

        rec = [dram(f"rec{k}", (EP, 4), I32) for k in range(3)]
        st = ExitStack()
        EC = 125
        this = sb(st, "this", [EC, E // EC], I32)
        after = sb(st, "after", [EC, E // EC], I32)
        fall = sb(st, "fall", [EC, E // EC])
        falls = sb(st, "falls", [EC, 1])
        cols4 = sb(st, "cols4", [P, T, 4], I32)
        one_col = sb(st, "one_col", [P, T], I32)
        tile4 = sb(st, "tile4", [P, 4], I32)
        digit = sb(st, "digit", [P, 1], I32)
        digit_f = sb(st, "digit_f", [P, 1])
        hot = sb(st, "hot", [P, P])
        run = sb(st, "run", [P, P])
        incl = sb(st, "incl", [P, P])
        none = sb(st, "none", [P, P])
        before = sb(st, "before", [P, P])
        pos_f = sb(st, "pos_f", [P, 1])
        pos = sb(st, "pos", [P, 1], I32)
        ps_s = ps(st, "ps_s", [P, 512])
        s_cmp = sem("compare_loaded")
        s_chk = sem("falls_counted")
        s_flag = sem("fall_total")
        s_uns = sem("order_known")
        s_cl = sem("sort_columns_loaded")
        s_cc = sem("sort_columns_packed")
        s_rw = sem("records_written")
        s_tl = sem("record_tile_loaded")
        s_tu = sem("record_tile_used")
        s_hot = sem("digit_onehot_ready")
        s_cnt = sem("digit_counted")
        s_schain = sem("sort_chain")
        s_pos = sem("places_ready")
        s_move = sem("records_scattered")
        block = nc.Block()
        with block:
            @block.sync
            def _(sp):
                sp.dma_start(this[:], dst_flat[0:E].rearrange("(p m) -> p m", p=EC)).then_inc(s_cmp, 16)
                sp.dma_start(after[:], dst_flat[1:E + 1].rearrange("(p m) -> p m", p=EC)).then_inc(s_cmp, 16)

            @block.vector
            def _(dve):
                dve.wait_ge(s_cmp, 32)
                dve.tensor_tensor(fall[:], this[:], after[:], ALU.is_gt).then_inc(s_chk, 1)
                dve.wait_ge(s_chk, 1)
                dve.tensor_reduce(falls[:], fall[:], X, ALU.max).then_inc(s_chk, 1)
                dve.wait_ge(s_flag, 1)
                dve.tensor_copy(unsorted[:], ps_s[0:1, 0:1]).then_inc(s_uns, 1)
                dve.wait_ge(s_uns, 1)

            @block.tensor
            def _(pe):
                pe.wait_ge(s_chk, 2)
                pe.matmul(ps_s[0:1, 0:1], falls[:], con[0:EC, C_ONES:C_ONES + 1], start=True,
                          stop=True).then_inc(s_flag, 1)
        PASSES = ((0, 0, 1), (7, 1, 2))
        block = nc.Block()
        with block:
            def found_unsorted(eng):
                return eng.value_load(unsorted[0:1, 0:1], min_val=0, max_val=EC) > 0

            @block.sync
            def _(sp):
                with sp.If(found_unsorted(sp)):
                    sp.wait_ge(s_cc, 1)
                    sp.dma_start(dst_flat[E:EP].rearrange("(a b) -> a b", a=1),
                                 one_col[0:1, 0:EP - E]).then_inc(s_rw, 16)
                    sp.wait_ge(s_rw, 16)
                    for n, flat in enumerate((src_flat, dst_flat, wgt_flat.bitcast(I32))):
                        sp.wait_ge(s_cc, 1 + n)
                        sp.dma_start(one_col[:], flat.rearrange("(p m) -> p m", p=P)).then_inc(s_cl, 16)
                    sp.wait_ge(s_cc, 4)
                    sp.dma_start(rec[0].rearrange("(p m) c -> p m c", p=P), cols4[:]).then_inc(s_rw, 16)
                    sp.wait_ge(s_rw, 32)
                    for n, (_, a, _) in enumerate(PASSES):
                        for half in range(2):
                            with sp.Fori(0, T) as i:
                                turn = (2 * n + half) * T + i
                                hold(sp, s_tu, turn + 1)
                                sp.dma_start(tile4[:], rec[a][bass.ds(i * P, P), :]).then_inc(s_tl, 16)
                        sp.wait_ge(s_move, 16 * T * (n + 1))
                    sp.dma_start(cols4[:], rec[2].rearrange("(p m) c -> p m c", p=P)).then_inc(s_cl, 16)
                    for n, flat in enumerate((src_flat, dst_flat, wgt_flat.bitcast(I32))):
                        sp.wait_ge(s_cc, 5 + n)
                        sp.dma_start(flat.rearrange("(p m) -> p m", p=P), one_col[:]).then_inc(s_rw, 16)
                        sp.wait_ge(s_rw, 48 + 16 * n)
                    for n, flat in enumerate((src_flat, dst_flat)):
                        sp.dma_start(flat[E:EP].rearrange("(a b) -> a b", b=1),
                                     flat[E - 1:E].partition_broadcast(EP - E)).then_inc(s_rw, 16)
                    sp.wait_ge(s_rw, 112)

            @block.vector
            def _(dve):
                with dve.If(found_unsorted(dve)):
                    dve.memset(cols4[:], 0)
                    dve.memset(none[:], 0.0)
                    dve.memset(one_col[:], P * P - 1).then_inc(s_cc, 1)
                    for n in range(3):
                        dve.wait_ge(s_cl, 16 * (n + 1))
                        dve.tensor_copy(cols4[:, :, n].bitcast(F32), one_col[:].bitcast(F32)).then_inc(s_cc, 1)
                        dve.wait_ge(s_cc, n + 2)
                    dve.sem_inc(s_tu, 1)
                    for n, (shift, _, _) in enumerate(PASSES):
                        dve.memset(run[:], 0.0).then_inc(s_schain, 1)
                        for half in range(2):
                            with dve.Fori(0, T) as i:
                                turn = (2 * n + half) * T + i
                                at = turn * 3 + (n * 3 + half * 2 + 1)

                                def link(instruction, k):
                                    instruction.then_inc(s_schain, 1)
                                    hold(dve, s_schain, at + k)

                                hold(dve, s_tl, turn * 16 + 16)
                                link(dve.tensor_scalar(digit[:], tile4[:, 1:2], shift, P - 1,
                                                       ALU.arith_shift_right, ALU.bitwise_and), 1)
                                link(dve.tensor_copy(digit_f[:], digit[:]), 2)
                                dve.tensor_scalar(hot[:], iota, digit_f[:], None, ALU.is_equal).then_inc(s_hot, 1)
                                hold(dve, s_cnt, turn + 1)
                                if half == 0:
                                    link(dve.tensor_tensor(run[:], run[:], ps_s[:, 0:P], ALU.add), 3)
                                    dve.sem_inc(s_tu, 1)
                                else:
                                    dve.tensor_tensor(before[:], run[:], ps_s[:, P:2 * P], ALU.add)
                                    link(dve.tensor_tensor(run[:], run[:], ps_s[:, 0:P], ALU.add), 3)
                                    hold(dve, s_uns, 1)
                                    dve.tensor_tensor_reduce(
                                        out=incl[:], in0=before[:], in1=hot[:], scale=1.0, scalar=0.0,
                                        op0=ALU.mult, op1=ALU.add, accum_out=pos_f[:]).then_inc(s_uns, 1)
                                    hold(dve, s_uns, n * T + i + 2)
                                    dve.tensor_copy(pos[:], pos_f[:]).then_inc(s_pos, 1)
                                    hold(dve, s_move, (n * T + i + 1) * 16)
                                    dve.sem_inc(s_tu, 1)
                            if half == 0:
                                dve.tensor_tensor_scan(incl[:], run[:], none[:], 0.0, ALU.add,
                                                       ALU.add).then_inc(s_schain, 1)
                                dve.wait_ge(s_schain, (2 * n + 1) * T * 3 + n * 3 + 2)
                                dve.tensor_tensor(run[:], incl[:], run[:], ALU.subtract).then_inc(s_schain, 1)
                                dve.wait_ge(s_schain, (2 * n + 1) * T * 3 + n * 3 + 3)
                    dve.wait_ge(s_cl, 64)
                    for n in range(3):
                        if n:
                            dve.wait_ge(s_rw, 32 + 16 * n)
                        dve.tensor_copy(one_col[:].bitcast(F32), cols4[:, :, n].bitcast(F32)).then_inc(s_cc, 1)

            @block.tensor
            def _(pe):
                with pe.If(found_unsorted(pe)):
                    with pe.Fori(0, 4 * T) as i:
                        hold(pe, s_hot, i + 1)
                        pe.matmul(ps_s[:, 0:P], con[:, C_ONES:C_ONES + P], hot[:], start=True, stop=True)
                        pe.matmul(ps_s[:, P:2 * P], con[:, C_TRI:C_TRI + P], hot[:], start=True,
                                  stop=True).then_inc(s_cnt, 1)

            @block.gpsimd
            def _(pool):
                with pool.If(found_unsorted(pool)):
                    for n, (_, _, b) in enumerate(PASSES):
                        with pool.Fori(0, T) as i:
                            hold(pool, s_pos, n * T + i + 1)
                            pool.indirect_dma_start(
                                rec[b], bass.IndirectOffsetOnAxis(ap=pos[:, 0:1], axis=0), tile4[:], None
                            ).then_inc(s_move, 16)
        st.close()

        st = ExitStack()
        dst_c = sb(st, "dst_c", [P, T])
        rows_i = sb(st, "rows_i", [P, 13, P], I32)
        rows_f = sb(st, "rows_f", [P, 13, P])
        tmp_i = sb(st, "tmp_i", [P, T], I32)
        lo_b = sb(st, "lo_b", [P, T], BF16)
        lo_h = sb(st, "lo_h", [P, T], I16)
        wide = sb(st, "wide", [1, NG])
        wide1 = sb(st, "wide1", [1, 2])
        base_b = sb(st, "base_b", [P, NG])
        last = sb(st, "last", [P, NG])
        ps_t = ps(st, "ps_t", [P, 4, 512])
        ps_b = ps(st, "ps_b", [P, 512])
        cols = ps_t[:, :, :].rearrange("p a b -> p (a b)")[:, 0:T]
        s_rows = sem("rows_loaded")
        s_rowf = sem("rows_as_floats")
        s_cols = sem("rows_transposed")
        s_free = sem("columns_copied")
        s_flat = sem("flat_loaded")
        s_lo = sem("low_bits_ready")
        s_los = sem("low_bits_stored")
        s_base = sem("bases_broadcast")

        def load_rows(sp, tile, flat, semaphore):
            sp.dma_start(tile[:, 0:12, :],
                         flat[0:12 * P * P].rearrange("(k r e) -> r k e", k=12, r=P)).then_inc(semaphore, 16)
            sp.dma_start(tile[0:TR, 12, :],
                         flat[12 * P * P:EP].rearrange("(r e) -> r e", r=TR)).then_inc(semaphore, 16)

        def transpose_rows(pe, rows, columns, done):
            for k, r in PIECES:
                last_one = pe.transpose(columns[:, k * P:k * P + r], rows[0:r, k, :], ident[0:r, 0:r])
            last_one.then_inc(done, 1)

        block = nc.Block()
        with block:
            @block.sync
            def _(sp):
                load_rows(sp, rows_i, src_flat, s_rows)
                sp.wait_ge(s_rowf, 1)
                load_rows(sp, rows_i, dst_flat, s_rows)
                sp.wait_ge(s_free, 2)
                load_rows(sp, rows_f, wgt_flat, s_rows)
                for n, flat in enumerate((src_flat, dst_flat)):
                    sp.wait_ge(s_free, 3 + n)
                    sp.dma_start(tmp_i[:], flat.rearrange("(p m) -> p m", p=P)).then_inc(s_flat, 16)
                    sp.wait_ge(s_lo, n + 1)
                    sp.dma_start((lo_src_flat, lo_dst_flat)[n].rearrange("(p m) -> p m", p=P),
                                 lo_b[:]).then_inc(s_los, 16)
                    if n == 0:
                        sp.dma_start(src16_flat.rearrange("(p m) -> p m", p=P), lo_h[:]).then_inc(s_los, 16)
                sp.wait_ge(s_los, 48)

            @block.vector
            def _(dve):
                link = Chain(dve, "edge_chain")
                for n, (as_float, hi) in enumerate(((src_c, hi_src), (dst_c, hi_dst))):
                    dve.wait_ge(s_rows, 32 * (n + 1))
                    if n:
                        dve.wait_ge(s_cols, n)
                    dve.tensor_copy(rows_f[:, 0:12, :], rows_i[:, 0:12, :])
                    dve.tensor_copy(rows_f[0:TR, 12, :], rows_i[0:TR, 12, :]).then_inc(s_rowf, 1)
                    dve.wait_ge(s_cols, n + 1)
                    dve.tensor_copy(as_float[:], cols)
                    ints = src_i if n == 0 else tmp_i
                    link(dve.tensor_copy(ints[:], cols))
                    link(dve.tensor_scalar(tmp_i[:], ints[:], 7, None, ALU.arith_shift_right))
                    link(dve.tensor_copy(hi[:], tmp_i[:]))
                    dve.sem_inc(s_free, 1)
                dve.wait_ge(s_cols, 3)
                dve.tensor_copy(w_c[:], cols)
                dve.wait_ge(s_base, 2)
                link(dve.tensor_copy(base_b[:], ps_b[:, 0:NG]))
                grouped = dl[:, :].rearrange("p (g j) -> p g j", j=GT)
                link(dve.tensor_tensor(grouped, dst_c[:, :].rearrange("p (g j) -> p g j", j=GT),
                                       base_b[:, :].unsqueeze(2).broadcast_to([P, NG, GT]), ALU.subtract))
                dve.tensor_copy(base_i[:], base_b[0:1, :])
                link(dve.tensor_scalar(neg_dl[:], dl[:], -1.0, None, ALU.mult))
                link(dve.tensor_tensor(wide[:], ps_b[0:1, NG:2 * NG], base_b[0:1, :], ALU.subtract))
                link(dve.tensor_reduce(wide1[:, 0:1], wide[:], X, ALU.max))
                link(dve.tensor_copy(tmp_i[0:1, 0:1], wide1[:, 0:1]))
                link(dve.tensor_scalar(tmp_i[0:1, 0:1], tmp_i[0:1, 0:1], 7, None, ALU.arith_shift_right))
                link(dve.tensor_copy(wide1[:, 0:1], tmp_i[0:1, 0:1]))
                link(dve.tensor_scalar(passes[:], wide1[:, 0:1], 1.0, None, ALU.add))
                dve.sem_inc(s_free, 1)
                for n in range(2):
                    dve.wait_ge(s_flat, 16 * (n + 1))
                    if n:
                        dve.wait_ge(s_los, 32)
                    if n == 0:
                        dve.tensor_copy(lo_h[:], tmp_i[:])
                    link(dve.tensor_scalar(tmp_i[:], tmp_i[:], 127, None, ALU.bitwise_and))
                    link(dve.tensor_copy(lo_b[:], tmp_i[:]))
                    dve.sem_inc(s_free, 1)
                    dve.sem_inc(s_lo, 1)

            @block.tensor
            def _(pe):
                for n in range(3):
                    if n < 2:
                        pe.wait_ge(s_rowf, n + 1)
                    else:
                        pe.wait_ge(s_rows, 96)
                    if n:
                        pe.wait_ge(s_free, n)
                    transpose_rows(pe, rows_f, cols, s_cols)
                ends = dst_c[:, :].rearrange("p (g j) -> p g j", j=GT)
                pe.matmul(ps_b[:, 0:NG], con[:, C_ROW0:C_ROW0 + P], ends[:, :, 0],
                          start=True, stop=True).then_inc(s_base, 1)
                pe.matmul(ps_b[0:1, NG:2 * NG], con[:, C_ID + P - 1:C_ID + P], ends[:, :, GT - 1],
                          start=True, stop=True).then_inc(s_base, 1)
        st.close()

        def norm_vector(dve, i, xins, t, s):
            for q, xin in enumerate(xins):
                if s["in"] is not None:
                    hold(dve, s["in"], i * 2 + q + 1)
                dve.tensor_reduce(t[q]["mean"][:], xin, X, ALU.add).then_inc(s["chain"], 1)
            for q, xin in enumerate(xins):
                hold(dve, s["chain"], i * 4 + q + 1)
                dve.scalar_tensor_tensor(t[q]["xc"][:], t[q]["mean"][:, :].unsqueeze(2).broadcast_to([P, CB, D]),
                                         -1.0 / D, xin, ALU.mult, ALU.add).then_inc(s["centred"], 1)
            for q in range(2):
                hold(dve, s["squared"], i * 2 + q + 1)
                dve.tensor_reduce(t[q]["var"][:], t[q]["sq"][:], X, ALU.add).then_inc(s["summed"], 1)
            for q in range(2):
                hold(dve, s["rooted"], i * 2 + q + 1)
                dve.reciprocal(t[q]["std"][:], t[q]["std"][:]).then_inc(s["chain"], 1)

        def norm_relu(dve, i, q, to, t, s):
            hold(dve, s["chain"], i * 4 + q + 3)
            return dve.scalar_tensor_tensor(to, t[q]["xc"][:], 0.0,
                                            t[q]["std"][:, :].unsqueeze(2).broadcast_to([P, CB, D]),
                                            ALU.max, ALU.mult)

        def norm_scalar(act, i, t, s):
            for q in range(2):
                hold(act, s["centred"], i * 2 + q + 1)
                act.activation(t[q]["sq"][:], t[q]["xc"][:], ACT.Square).then_inc(s["squared"], 1)
            for q in range(2):
                hold(act, s["summed"], i * 2 + q + 1)
                act.activation(t[q]["std"][:], t[q]["var"][:], ACT.Sqrt, bias=con[:, C_EPS:C_EPS + 1],
                               scale=1.0 / D).then_inc(s["rooted"], 1)

        def norm_tiles(stack, name):
            return [{"mean": sb(stack, f"{name}_mean{q}", [P, CB]), "var": sb(stack, f"{name}_var{q}", [P, CB]),
                     "std": sb(stack, f"{name}_std{q}", [P, CB]), "xc": sb(stack, f"{name}_xc{q}", [P, CB, D]),
                     "sq": sb(stack, f"{name}_sq{q}", [P, CB, D])} for q in range(2)]

        def norm_sems(name):
            return {k: sem(name + "_" + k) for k in ("chain", "centred", "squared", "summed", "rooted")}

        st = ExitStack()
        t = norm_tiles(st, "n0")
        h = [sb(st, f"h{q}", [P, CB, D]) for q in range(2)]
        ht = [sb(st, f"ht{q}", [P, CW]) for q in range(2)]
        h_out = [sb(st, f"h_out{q}", [P, CB, D]) for q in range(2)]
        w_t = sb(st, "w_t", [P, D])
        a_cols = sb(st, "a_cols", [P, 2])
        ps_ht = [ps(st, f"ps_ht{q}", [P, 1024]) for q in range(2)]
        ps_h = [ps(st, f"ps_h{q}", [P, 1024]) for q in range(2)]
        PAIR = slice(CW, CW + 2 * CB)
        s = norm_sems("n0")
        s["in"] = None
        s_w = sem("w0_loaded")
        s_wt = sem("w0_transposed")
        s_wtc = sem("w0_transpose_copied")
        s_wa = sem("w0_times_a")
        s_wext = sem("w0_extended")
        s_h = sem("h_normed")
        s_tp = sem("h_transposed")
        s_htc = sem("h_transpose_copied")
        s_hw = sem("h_projected")
        s_hwc = sem("h_projection_copied")
        s_hfree = sem("h_out_stored")
        block = nc.Block()
        with block:
            @block.sync
            def _(sp):
                sp.dma_start(wext[:, 0:D], w0).then_inc(s_w, 16)
                sp.dma_start(a_cols[:, 0:1], a_src.rearrange("(p a) -> p a", a=1)).then_inc(s_w, 16)
                sp.dma_start(a_cols[:, 1:2], a_dst.rearrange("(p a) -> p a", a=1)).then_inc(s_w, 16)
                sp.dma_start(bias0_col[:], bias0.rearrange("(p a) -> p a", a=1)).then_inc(s_w, 16)
                sp.sem_inc(s_hfree, 16)
                table = h_table.rearrange("(b p) f -> p b f", p=P)
                with sp.Fori(0, NC // 2) as i:
                    for q in range(2):
                        hold(sp, s_hwc, i * 2 + q + 1)
                        sp.dma_start(table[:, bass.ds((i * 2 + q) * CB, CB), :], h_out[q][:]).then_inc(s_hfree, 16)
                sp.wait_ge(s_hfree, 16 * (NC + 1))

            @block.vector
            def _(dve):
                dve.wait_ge(s_wt, 1)
                dve.tensor_copy(w_t[:], ps_h[0][:, 0:D]).then_inc(s_wtc, 1)
                dve.wait_ge(s_wa, 1)
                dve.tensor_copy(wext[:, D:D + 2], ps_h[0][:, D:D + 2]).then_inc(s_wext, 1)
                dve.wait_ge(s_x, 32)
                with dve.Fori(0, NC // 2) as i:
                    norm_vector(dve, i, [x_sb[:, bass.ds((i * 2 + q) * CB, CB), :] for q in range(2)], t, s)
                    for q in range(2):
                        norm_relu(dve, i, q, h[q][:], t, s).then_inc(s_h, 1)

            @block.scalar
            def _(act):
                with act.Fori(0, NC // 2) as i:
                    norm_scalar(act, i, t, s)
                    for q in range(2):
                        hold(act, s_tp, i * 2 + q + 1)
                        act.activation(ht[q][:], ps_ht[q][:, 0:CW], ACT.Copy).then_inc(s_htc, 1)
                    hold(act, s_hfree, i * 32 + 16)
                    for q in range(2):
                        hold(act, s_hw, i * 2 + q + 1)
                        pair = ps_h[q][:, PAIR].rearrange("p (b k) -> p b k", k=2)
                        act.activation(es_tab[:, bass.ds((i * 2 + q) * CB, CB)], pair[:, :, 0], ACT.Copy)
                        act.activation(ed_tab[:, bass.ds((i * 2 + q) * CB, CB)], pair[:, :, 1], ACT.Copy)
                        act.activation(h_out[q][:, :, :].rearrange("p b f -> p (b f)"), ps_h[q][:, 0:CW],
                                       ACT.Copy).then_inc(s_hwc, 1)

            @block.tensor
            def _(pe):
                pe.wait_ge(s_w, 64)
                pe.transpose(ps_h[0][:, 0:D], wext[:, 0:D], ident).then_inc(s_wt, 1)
                pe.wait_ge(s_wtc, 1)
                pe.matmul(ps_h[0][:, D:D + 2], w_t[:], a_cols[:], start=True, stop=True).then_inc(s_wa, 1)
                pe.wait_ge(s_wext, 1)
                with pe.Fori(0, NC // 2) as i:
                    for q in range(2):
                        hold(pe, s_h, i * 2 + q + 1)
                        for j in range(CB):
                            tp = pe.transpose(ps_ht[q][:, j * P:(j + 1) * P], h[q][:, j, :], ident)
                        tp.then_inc(s_tp, 1)
                    for q in range(2):
                        hold(pe, s_htc, i * 2 + q + 1)
                        for j in range(CB):
                            pe.matmul(ps_h[q][:, j * P:(j + 1) * P], ht[q][:, j * P:(j + 1) * P], wext[:, 0:D],
                                      start=True, stop=True)
                            mm = pe.matmul(ps_h[q][:, CW + 2 * j:CW + 2 * j + 2], ht[q][:, j * P:(j + 1) * P],
                                           wext[:, D:D + 2], start=True, stop=True)
                        mm.then_inc(s_hw, 1)
        st.close()

        xs.close()

        agg_stack = ExitStack()
        agg = sb(agg_stack, "agg", [P, AW])
        st = ExitStack()
        RING = 7
        tabs = [[sb(st, f"tab{a}{k}", [P, NB], BF16) for k in range(3)] for a in range(2)]
        rest = sb(st, "rest", [P, NB])
        lo_rows = [[sb(st, f"lo_rows{q}{a}", [P, GT * P], BF16) for a in range(2)] for q in range(2)]
        onehot = [[sb(st, f"onehot{q}{a}", [P, GT * P], BF16) for a in range(2)] for q in range(2)]
        picked = sb(st, "picked", [P, 2 * GT, NB])
        es_c = sb(st, "es_c", [P, CT])
        ed_c = sb(st, "ed_c", [P, CT])
        alpha = sb(st, "alpha", [P, CT])
        neg_alpha = sb(st, "neg_alpha", [P, CT])
        windows = sb(st, "windows", [P, AW], I16)
        stage = [sb(st, f"stage{r}", [P, GT], I32) for r in range(RING)]
        gath = sb(st, "gath", [P, RING, GT, D])
        spread = sb(st, "spread", [P, 2 * GT, W])
        row_i = sb(st, "row_i", [CT, P], I32)
        R = {k: sb(st, "row_" + k, [CT, P]) for k in
             ("dst", "es", "ed", "same", "next", "a", "b", "m", "p", "e", "ramp")}
        ramp_i = sb(st, "ramp_i", [CT, P], I32)
        ends = sb(st, "ends", [CT, 4])
        carry = sb(st, "carry", [CT, 2])
        L = {k: sb(st, "line_" + k, [1, CT + 2]) for k in
             ("head", "tail", "hv", "tv", "cont", "whole", "d0", "d1", "cin", "cout", "pc", "pw")}
        C = {k: sb(st, "cell_" + k, [1, 1]) for k in ("max", "den", "shift", "scaled", "rec", "f", "keep")}
        factor = sb(st, "factor", [P, 1])
        ZC = 18
        zero_tile = sb(st, "zero_tile", [P, AW * RW // P // ZC])
        ps_pick = [ps(st, f"ps_pick{b}", [P, 4, P]) for b in range(4)]
        ps_w = [ps(st, f"ps_w{q}", [P, 512]) for q in range(2)]
        ps_r = ps(st, "ps_r", [P, 512])
        ps_l = ps(st, "ps_l", [P, 512])
        s_lor = [sem(f"low_rows_loaded{q}") for q in range(2)]
        s_oh = sem("onehots_ready")
        s_pk = [sem(f"rows_picked{b}") for b in range(4)]
        s_sel = [sem(f"columns_picked{b}") for b in range(4)]
        s_stage = sem("indices_staged")
        s_rfree = sem("gathered_rows_used")
        s_gath = [sem(f"rows_gathered{r}") for r in range(RING)]
        s_dist = sem("distances_ready")
        s_spread = sem("spread_ready")
        s_win = sem("window_summed")
        s_added = sem("window_added")
        s_setup = sem("layer0_set_up")
        s_wins = sem("windows_numbered")
        s_row = sem("destination_rows_loaded")
        s_rowu = sem("destination_rows_used")
        s_sc = sem("softmax_chain")
        s_ask = sem("softmax_asks_tensor")
        s_ans = sem("tensor_answers_softmax")
        s_eask = sem("softmax_asks_exponential")
        s_eans = sem("exponential_answers_softmax")
        s_alpha = sem("alpha_ready")
        block = nc.Block()
        with block:
            def buf(s):
                return s % 2

            def pass_count(eng):
                return eng.value_load(passes[0:1, 0:1], min_val=1, max_val=NB + 1)

            def last_use(turn, n_pass):
                return turn + 2 + (n_pass > 1)

            @block.sync
            def _(sp):
                with sp.Fori(0, NCH) as c:
                    for s in range(CG):
                        hold(sp, s_oh, c * CG + s + 1)
                        for a, flat in enumerate((lo_src_flat, lo_dst_flat)):
                            sp.dma_start(lo_rows[buf(s)][a][:],
                                         flat[bass.ds((c * CG + s) * GT * P, GT * P)].partition_broadcast(P)
                                         ).then_inc(s_lor[buf(s)], 16)
                    hold(sp, s_rowu, c + 1)
                    sp.dma_start(row_i[:], dst_flat[bass.ds(c * CT * P, CT * P)].rearrange("(r e) -> r e", e=P)
                                 ).then_inc(s_row, 16)

            @block.gpsimd
            def _(pool):
                pool.iota(ramp_i[:], pattern=[[1, P]], base=0, channel_multiplier=P).then_inc(s_wins, 1)
                pool.iota(windows[:], pattern=[[1, AW]], base=0, channel_multiplier=0).then_inc(s_wins, 1)
                with pool.Fori(0, NG // RING) as body:
                    for s in range(RING):
                        hold(pool, s_stage, body * RING + s + 1)
                        for j in range(GT):
                            pool.indirect_dma_start(
                                gath[:, s, j, :], None, h_table,
                                bass.IndirectOffsetOnAxis(ap=stage[s][:, j:j + 1], axis=0)
                            ).then_inc(s_gath[s], 16)

            @block.vector
            def _(dve):
                first = Chain(dve, "split_chain")
                for a, tab in enumerate((es_tab, ed_tab)):
                    first(dve.tensor_copy(tabs[a][0][:], tab[:]))
                    first(dve.tensor_tensor(rest[:], tab[:], tabs[a][0][:], ALU.subtract))
                    first(dve.tensor_copy(tabs[a][1][:], rest[:]))
                    first(dve.tensor_tensor(rest[:], rest[:], tabs[a][1][:], ALU.subtract))
                    first(dve.tensor_copy(tabs[a][2][:], rest[:]))
                dve.memset(zero_tile[:], 0.0).then_inc(s_zt, 1)
                dve.memset(agg[:], 0.0).then_inc(s_added, 1)
                dve.sem_inc(s_added, 2)
                dve.memset(C["max"][:], -BIG)
                dve.memset(C["den"][:], 0.0)
                dve.memset(L["tail"][:], -1.0)
                dve.wait_ge(s_wins, 1)
                first(dve.tensor_copy(R["ramp"][:], ramp_i[:]))
                dve.sem_inc(s_oh, 2)
                dve.sem_inc(s_rowu, 1)
                n_pass = pass_count(dve)

                def make_onehots(c, s):
                    q = buf(s)
                    hold(dve, s_lor[q], c * (CG // 2 * 32) + (s // 2 * 32 + 32))
                    for a in range(2):
                        oh = dve.tensor_scalar(onehot[q][a][:], lo_rows[q][a][:], con[:, C_PART:C_PART + 1],
                                               None, ALU.is_equal)
                    oh.then_inc(s_oh, 1)

                def pick(c, s, banks):
                    for b in banks:
                        hold(dve, s_pk[b], c * CG + s + 1)
                        hi, to = ((hi_src, es_c), (hi_dst, ed_c))[b // 2]
                        for j in range(4):
                            tile = (b % 2) * 4 + j
                            sel = dve.scalar_tensor_tensor(
                                picked[:, (b // 2) * GT + tile, :], iota[:, 0:NB],
                                hi[:, bass.ds((c * CG + s) * GT + tile, 1)], ps_pick[b][:, j, 0:NB],
                                ALU.is_equal, ALU.mult, accum_out=to[:, s * GT + tile:s * GT + tile + 1])
                        sel.then_inc(s_sel[b], 1)

                def add_window(g, s):
                    base = dve.value_load(base_i[0:1, bass.ds(g, 1)], min_val=0, max_val=NP)
                    with dve.Fori(0, n_pass) as k:
                        turn = g * n_pass + k
                        at = base + k * W
                        at = (at * (at <= NP)).with_bounds(min_val=0, max_val=NP)
                        here = agg[:, bass.ds(at, W)]
                        hold(dve, s_win, turn + 4)
                        hold(dve, s_added, turn + 3)
                        dve.tensor_tensor(here, here, ps_w[buf(s)][:, 0:W], ALU.add).then_inc(s_added, 1)
                    dve.sem_inc(s_rfree, 1)

                def softmax(c):
                    rev = slice(None, None, -1)
                    count = [0]

                    def link(instruction):
                        count[0] += 1
                        instruction.then_inc(s_sc, 1)
                        dve.wait_ge(s_sc, count[0])

                    asks = [0]

                    def ask():
                        asks[0] += 1
                        dve.sem_inc(s_ask, 1)

                    def answer():
                        hold(dve, s_ans, c * 6 + asks[0])

                    def first_part(x):
                        return x[:, 1:CT + 1]

                    dve.sem_clear(s_sc)
                    link(dve.tensor_copy(C["keep"][:], L["tail"][:, CT:CT + 1]))
                    hold(dve, s_row, c * 16 + 16)
                    link(dve.tensor_copy(R["dst"][:], row_i[:]))
                    dve.sem_inc(s_rowu, 1)
                    ask()
                    yield
                    answer()
                    dve.tensor_copy(R["es"][:], ps_r[0:CT, 0:P])
                    dve.tensor_copy(R["ed"][:], ps_r[0:CT, P:2 * P])
                    dstr, same, nxt, a, b, m = (R[k] for k in ("dst", "same", "next", "a", "b", "m"))
                    dve.memset(same[:, 0:1], 0.0)
                    dve.memset(nxt[:, P - 1:P], 0.0)
                    dve.tensor_tensor(same[:, 1:P], dstr[:, 1:P], dstr[:, 0:P - 1], ALU.is_equal)
                    link(dve.tensor_tensor(nxt[:, 0:P - 1], dstr[:, 1:P], dstr[:, 0:P - 1], ALU.is_equal))
                    link(dve.tensor_scalar(b[:], same[:], 1.0, BIG, ALU.subtract, ALU.mult))
                    link(dve.tensor_tensor_scan(a[:], b[:], R["es"][:], -BIG, ALU.add, ALU.max))
                    link(dve.tensor_scalar(b[:], nxt[:], 1.0, BIG, ALU.subtract, ALU.mult))
                    link(dve.tensor_tensor_scan(m[:, rev], b[:, rev], a[:, rev], -BIG, ALU.add, ALU.max))
                    dve.tensor_copy(ends[:, 0:1], dstr[:, 0:1])
                    dve.tensor_copy(ends[:, 1:2], dstr[:, P - 1:P])
                    dve.tensor_copy(ends[:, 2:3], m[:, 0:1])
                    link(dve.tensor_copy(ends[:, 3:4], a[:, P - 1:P]))
                    ask()
                    yield
                    answer()
                    for k, name in enumerate(("head", "tail", "hv", "tv")):
                        dve.tensor_copy(first_part(L[name]), ps_l[0:1, k * CT:(k + 1) * CT])
                    dve.tensor_copy(L["head"][:, 0:1], C["keep"][:])
                    dve.tensor_copy(L["tail"][:, 0:1], C["keep"][:])
                    dve.tensor_copy(L["hv"][:, 0:1], C["max"][:])
                    link(dve.tensor_copy(L["tv"][:, 0:1], C["max"][:]))
                    rows_all, prev, nextr = slice(1, CT + 1), slice(0, CT), slice(2, CT + 1)
                    dve.tensor_tensor(L["cont"][:, rows_all], L["head"][:, rows_all], L["tail"][:, prev],
                                      ALU.is_equal)
                    dve.memset(L["cont"][:, CT + 1:CT + 2], 1.0)
                    link(dve.tensor_tensor(L["whole"][:, 0:CT + 1], L["head"][:, 0:CT + 1],
                                           L["tail"][:, 0:CT + 1], ALU.is_equal))
                    link(dve.tensor_scalar(L["pc"][:, 1:CT + 2], L["cont"][:, 1:CT + 2], 1.0, BIG,
                                           ALU.subtract, ALU.mult))
                    link(dve.tensor_scalar(L["pw"][:, 0:CT + 1], L["whole"][:, 0:CT + 1], 1.0, BIG,
                                           ALU.subtract, ALU.mult))

                    def carries(w, cont, nothing, join, scan):
                        dve.tensor_tensor(L["d0"][:, 1:CT + 2], w[:, 0:CT + 1], cont[:, 1:CT + 2], join)
                        link(dve.tensor_tensor(L["d1"][:, 1:CT + 2], L["tv"][:, 0:CT + 1], cont[:, 1:CT + 2], join))
                        link(dve.tensor_tensor_scan(L["cin"][:, 1:CT + 2], L["d0"][:, 1:CT + 2],
                                                    L["d1"][:, 1:CT + 2], nothing, join, scan))
                        dve.memset(L["d0"][:, CT:CT + 1], nothing)
                        dve.memset(L["d1"][:, CT:CT + 1], nothing)
                        dve.tensor_tensor(L["d0"][:, 1:CT], w[:, nextr], cont[:, nextr], join)
                        link(dve.tensor_tensor(L["d1"][:, 1:CT], L["hv"][:, nextr], cont[:, nextr], join))
                        link(dve.tensor_tensor_scan(L["cout"][:, CT:0:-1], L["d0"][:, CT:0:-1],
                                                    L["d1"][:, CT:0:-1], nothing, join, scan))

                    carries(L["pw"], L["pc"], -BIG, ALU.add, ALU.max)
                    ask()
                    yield
                    answer()
                    link(dve.tensor_copy(carry[:], ps_l[0:CT, 448:450]))
                    for k, end in enumerate((dstr[:, 0:1], dstr[:, P - 1:P])):
                        link(dve.tensor_scalar(b[:], dstr[:], end, -BIG, ALU.not_equal, ALU.mult))
                        link(dve.scalar_tensor_tensor(m[:], b[:], carry[:, k:k + 1], m[:], ALU.add, ALU.max))
                    dve.tensor_tensor(C["shift"][:], C["max"][:], R["ed"][0:1, 0:1], ALU.add)
                    dve.tensor_tensor(a[:], R["es"][:], R["ed"][:], ALU.add)
                    link(dve.tensor_tensor(m[:], m[:], R["ed"][:], ALU.add))
                    dve.tensor_copy(C["max"][:], L["cin"][:, CT + 1:CT + 2])
                    dve.scalar_tensor_tensor(C["scaled"][:], C["shift"][:], SLOPE, C["shift"][:], ALU.mult, ALU.max)
                    dve.scalar_tensor_tensor(b[:], a[:], SLOPE, a[:], ALU.mult, ALU.max)
                    link(dve.scalar_tensor_tensor(R["e"][:], m[:], SLOPE, m[:], ALU.mult, ALU.max))
                    dve.tensor_tensor(C["shift"][:], C["scaled"][:], R["e"][0:1, 0:1], ALU.subtract)
                    link(dve.tensor_tensor(b[:], b[:], R["e"][:], ALU.subtract))
                    link(dve.tensor_scalar(C["shift"][:], C["shift"][:], 0.0, None, ALU.min))
                    dve.sem_inc(s_eask, 1)
                    yield
                    hold(dve, s_eans, c + 1)
                    link(dve.scalar_tensor_tensor(R["p"][:], R["ramp"][:], float(E), R["e"][:], ALU.is_lt,
                                                  ALU.mult))
                    link(dve.tensor_scalar(R["ramp"][:], R["ramp"][:], float(CT * P), None, ALU.add))
                    link(dve.tensor_tensor_scan(a[:], same[:], R["p"][:], 0.0, ALU.mult, ALU.add))
                    link(dve.scalar_tensor_tensor(b[:], nxt[:], 0.0, a[:], ALU.is_equal, ALU.mult))
                    link(dve.tensor_tensor_scan(m[:, rev], nxt[:, rev], b[:, rev], 0.0, ALU.mult, ALU.add))
                    dve.tensor_copy(ends[:, 2:3], m[:, 0:1])
                    link(dve.tensor_copy(ends[:, 3:4], a[:, P - 1:P]))
                    link(dve.tensor_tensor(C["scaled"][:], C["scaled"][:], C["den"][:], ALU.mult))
                    ask()
                    yield
                    answer()
                    for k, name in ((2, "hv"), (3, "tv")):
                        dve.tensor_copy(first_part(L[name]), ps_l[0:1, k * CT:(k + 1) * CT])
                    dve.tensor_copy(L["hv"][:, 0:1], C["scaled"][:])
                    link(dve.tensor_copy(L["tv"][:, 0:1], C["scaled"][:]))
                    carries(L["whole"], L["cont"], 0.0, ALU.mult, ALU.add)
                    dve.tensor_copy(C["den"][:], L["cin"][:, CT + 1:CT + 2])
                    ask()
                    yield
                    answer()
                    link(dve.tensor_copy(carry[:], ps_l[0:CT, 448:450]))
                    for k, end in enumerate((dstr[:, 0:1], dstr[:, P - 1:P])):
                        link(dve.tensor_scalar(b[:], dstr[:], end, carry[:, k:k + 1], ALU.is_equal, ALU.mult))
                        link(dve.tensor_tensor(m[:], m[:], b[:], ALU.add))
                    link(dve.tensor_scalar(m[:], m[:], 1e-15, None, ALU.max))
                    link(dve.reciprocal(m[:], m[:]))
                    link(dve.tensor_tensor(a[:], R["p"][:], m[:], ALU.mult))
                    link(dve.tensor_tensor(C["f"][:], C["scaled"][:], m[0:1, 0:1], ALU.mult))
                    link(dve.tensor_scalar(C["f"][:], C["f"][:], -1.0, None, ALU.add))
                    link(dve.tensor_tensor(C["f"][:], C["f"][:], L["cont"][:, 1:2], ALU.mult))
                    link(dve.tensor_scalar(C["f"][:], C["f"][:], 1.0, None, ALU.add))
                    ask()
                    yield
                    answer()
                    dve.tensor_copy(alpha[:], ps_r[:, 256:256 + CT])
                    dve.tensor_scalar(neg_alpha[:], ps_r[:, 256:256 + CT], -1.0, None, ALU.mult)
                    link(dve.tensor_copy(factor[:], ps_r[:, 511:512]))
                    dve.sem_inc(s_alpha, 1)
                    base = dve.value_load(base_i[0:1, bass.ds(c * (2 * RING), 1)], min_val=0, max_val=NP)
                    column = agg[:, bass.ds(base, 1)]
                    hold(dve, s_added, c * (2 * RING) * n_pass + 3)
                    link(dve.tensor_scalar(column, column, factor[:], None, ALU.mult))
                    yield

                def chunk(add=None, norm=None, look=None):
                    if look is not None:
                        make_onehots(look, 0)
                        make_onehots(look, 1)
                    if norm is not None:
                        soft = softmax(norm)
                        next(soft)
                        next(soft)
                    for s in range(CG):
                        if look is not None:
                            if s > 0 and s + 1 < CG:
                                make_onehots(look, s + 1)
                            pick(look, s, range(2))
                        if add is not None:
                            add_window(add * CG + s, s)
                        if look is not None:
                            pick(look, s, range(2, 4))
                        if norm is not None and s in SOFTMAX_AT:
                            next(soft)
                    if norm is not None:
                        next(soft)

                chunk(look=0)
                chunk(norm=0, look=1)
                with dve.Fori(0, NCH - 2) as c:
                    chunk(add=c, norm=c + 1, look=c + 2)
                chunk(add=NCH - 2, norm=NCH - 1)
                chunk(add=NCH - 1)

            @block.scalar
            def _(act):
                act.wait_ge(s_zt, 2)
                n = AW * RW // P
                for k in range(NACC):
                    view = acc[k].rearrange("r c -> (r c)").rearrange("(p m) -> p m", p=P)
                    for j in range(ZC):
                        act.dma_start(view[:, j * (n // ZC):(j + 1) * (n // ZC)],
                                      zero_tile[:, :]).then_inc(s_zero, 16)
                act.dma_start(h2_table[NP:AW, :], zero_tile[:, 0:D]).then_inc(s_zero, 16)
                act.wait_ge(s_wins, 2)
                act.sem_inc(s_rfree, RING)
                n_pass = pass_count(act)

                def stage_indices(g, r):
                    hold(act, s_rfree, g + 1)
                    act.activation(stage[r][:], src_i[:, bass.ds(g * GT, GT)], ACT.Copy).then_inc(s_stage, 1)

                def make_spread(c, s):
                    q = buf(s)
                    with act.Fori(0, n_pass) as k:
                        turn = (c * CG + s) * n_pass + k
                        hold(act, s_win, last_use(turn, n_pass))
                        for j in range(GT):
                            far = act.activation(spread[:, q * GT + j, :], windows[:, bass.ds(k * W, W)], ACT.Abs,
                                                 bias=neg_dl[:, bass.ds((c * CG + s) * GT + j, 1)])
                        far.then_inc(s_dist, 1)
                        hold(act, s_dist, turn + 1)
                        for j in range(GT):
                            col = s * GT + j
                            sp_ = act.activation(spread[:, q * GT + j, :], spread[:, q * GT + j, :], ACT.Relu,
                                                 bias=alpha[:, col:col + 1], scale=neg_alpha[:, col:col + 1])
                        sp_.then_inc(s_spread, 1)

                def exponentials(c):
                    hold(act, s_eask, c + 1)
                    act.activation(C["scaled"][:], C["shift"][:], ACT.Exp)
                    act.activation(R["e"][:], R["b"][:], ACT.Exp).then_inc(s_eans, 1)

                for g in range(RING - 1):
                    stage_indices(g, g)
                exponentials(0)
                with act.Fori(0, NCH - 1) as c:
                    hold(act, s_alpha, c + 1)
                    for s in range(CG):
                        make_spread(c, s)
                        stage_indices(c * CG + (s + RING - 1), (s + RING - 1) % RING)
                        if s == EXPONENTIALS_AT:
                            exponentials(c + 1)
                hold(act, s_alpha, NCH)
                for s in range(CG):
                    make_spread(NCH - 1, s)
                    if s + RING - 1 < CG:
                        stage_indices((NCH - 1) * CG + (s + RING - 1), (s + RING - 1) % RING)
                act.wait_ge(s_zero, 16 * (ZC * NACC + 1))

            @block.tensor
            def _(pe):
                for b in range(4):
                    pe.sem_inc(s_sel[b], 1)
                pe.sem_inc(s_win, 3)
                n_pass = pass_count(pe)

                def lookup(c, s, banks):
                    q = buf(s)
                    hold(pe, s_oh, c * CG + s + 3)
                    for b in banks:
                        hold(pe, s_sel[b], c * CG + s + 1)
                        for j in range(4):
                            tile = (b % 2) * 4 + j
                            for k in range(3):
                                mm = pe.matmul(ps_pick[b][:, j, 0:NB],
                                               onehot[q][b // 2][:, tile * P:(tile + 1) * P],
                                               tabs[b // 2][k][:], start=(k == 0), stop=(k == 2))
                        mm.then_inc(s_pk[b], 1)

                def product(c, s):
                    q = buf(s)
                    hold(pe, s_gath[s % RING], (c * (CG // RING) + (s // RING + 1)) * (16 * GT))
                    with pe.Fori(0, n_pass) as k:
                        turn = (c * CG + s) * n_pass + k
                        hold(pe, s_spread, turn + 1)
                        hold(pe, s_added, last_use(turn, n_pass))
                        for j in range(GT):
                            mm = pe.matmul(ps_w[q][:, 0:W], gath[:, s % RING, j, :], spread[:, q * GT + j, :],
                                           start=(j == 0), stop=(j == GT - 1))
                        mm.then_inc(s_win, 1)

                def lines(which):
                    for k in which:
                        tp = pe.transpose(ps_l[0:1, k * CT:(k + 1) * CT], ends[:, k:k + 1], ident[0:CT, 0:CT])
                    tp.then_inc(s_ans, 1)

                def columns():
                    pe.transpose(ps_l[0:CT, 448:449], L["cin"][:, 1:CT + 1], ident[0:1, 0:1])
                    pe.transpose(ps_l[0:CT, 449:450], L["cout"][:, 1:CT + 1], ident[0:1, 0:1]).then_inc(s_ans, 1)

                def serve(c, n):
                    hold(pe, s_ask, c * 6 + n)
                    if n == 1:
                        pe.transpose(ps_r[0:CT, 0:P], es_c[:], ident)
                        pe.transpose(ps_r[0:CT, P:2 * P], ed_c[:], ident).then_inc(s_ans, 1)
                    elif n == 2:
                        lines(range(4))
                    elif n == 4:
                        lines((2, 3))
                    elif n in (3, 5):
                        columns()
                    else:
                        pe.transpose(ps_r[:, 256:256 + CT], R["a"][:], ident[0:CT, 0:CT])
                        pe.matmul(ps_r[:, 511:512], con[0:1, C_ONES:C_ONES + P], C["f"][:], start=True,
                                  stop=True).then_inc(s_ans, 1)

                def chunk(add=None, norm=None, look=None):
                    if norm is not None:
                        serve(norm, 1)
                    for s in range(CG):
                        if look is not None:
                            lookup(look, s, range(2))
                        if add is not None:
                            product(add, s)
                        if look is not None:
                            lookup(look, s, range(2, 4))
                        if norm is not None and s in QUESTION_AT:
                            serve(norm, QUESTION_AT[s])

                chunk(look=0)
                chunk(norm=0, look=1)
                with pe.Fori(0, NCH - 2) as c:
                    chunk(add=c, norm=c + 1, look=c + 2)
                chunk(add=NCH - 2, norm=NCH - 1)
                chunk(add=NCH - 1)
        st.close()

        st = ExitStack()
        t = norm_tiles(st, "n1")
        below = [sb(st, f"below{q}", [P, CW]) for q in range(2)]
        above = [sb(st, f"above{q}", [P, CW]) for q in range(2)]
        elu = [sb(st, f"elu{q}", [P, CW]) for q in range(2)]
        h2_out = [sb(st, f"h2_out{q}", [P, CB, D]) for q in range(2)]
        x_in = [sb(st, f"x_in{q}", [P, CB, D]) for q in range(2)]
        ps_x = [ps(st, f"ps_x{q}", [P, 1024]) for q in range(2)]
        s_xin = sem("x_chunk_loaded")
        s_xlast = sem("last_whole_blocks_loaded")
        s = norm_sems("n1")
        s_neg = sem("negative_part_ready")
        s_nexp = sem("negative_part_exponentiated")
        s_elu = sem("elu_ready")
        s_elut = sem("elu_transposed")
        s_in1 = sem("residual_added")
        s_h2 = sem("h2_normed")
        s_h2s = sem("h2_stored")
        s["in"] = s_in1
        block = nc.Block()
        with block:
            @block.vector
            def _(dve):
                with dve.Fori(0, NC // 2) as i:
                    parts = [agg[:, bass.ds((i * 2 + q) * CW, CW)] for q in range(2)]
                    rows = [part.rearrange("p (b f) -> p b f", f=D) for part in parts]
                    for q in range(2):
                        dve.tensor_scalar(below[q][:], parts[q], bias0_col[:], 0.0, ALU.add,
                                          ALU.min).then_inc(s_neg, 1)
                    for q in range(2):
                        hold(dve, s_nexp, i * 2 + q + 1)
                        dve.scalar_tensor_tensor(elu[q][:], below[q][:], -1.0, above[q][:], ALU.add,
                                                 ALU.add).then_inc(s_elu, 1)
                    hold(dve, s_xin, i * 32 + 32)
                    for q in range(2):
                        hold(dve, s_elut, i * 2 + q + 1)
                        dve.tensor_tensor(rows[q], x_in[q][:], ps_x[q][:, 0:CW].rearrange("p (b f) -> p b f", f=D),
                                          ALU.add).then_inc(s_in1, 1)
                    norm_vector(dve, i, rows, t, s)
                    hold(dve, s_h2s, i * 32 + 16)
                    for q in range(2):
                        norm_relu(dve, i, q, h2_out[q][:], t, s).then_inc(s_h2, 1)

            @block.scalar
            def _(act):
                with act.Fori(0, NC // 2) as i:
                    for q in range(2):
                        hold(act, s_neg, i * 2 + q + 1)
                        act.activation(above[q][:], agg[:, bass.ds((i * 2 + q) * CW, CW)], ACT.Relu,
                                       bias=bias0_col[:])
                        act.activation(below[q][:], below[q][:], ACT.Exp).then_inc(s_nexp, 1)
                    norm_scalar(act, i, t, s)

            @block.tensor
            def _(pe):
                with pe.Fori(0, NC // 2) as i:
                    for q in range(2):
                        hold(pe, s_elu, i * 2 + q + 1)
                        for j in range(CB):
                            tp = pe.transpose(ps_x[q][:, j * P:(j + 1) * P], elu[q][:, j * P:(j + 1) * P], ident)
                        tp.then_inc(s_elut, 1)

            @block.sync
            def _(sp):
                table = h2_table[0:NP, :].rearrange("(b p) f -> p b f", p=P)
                x_rows = x[0:(NB - 1) * P, :].rearrange("(b p) f -> p b f", p=P)
                sp.sem_inc(s_h2s, 16)

                def store(i):
                    for q in range(2):
                        hold(sp, s_h2, i * 2 + q + 1)
                        sp.dma_start(table[:, bass.ds((i * 2 + q) * CB, CB), :], h2_out[q][:]).then_inc(s_h2s, 16)

                for q in range(2):
                    sp.dma_start(x_in[q][:], x_rows[:, q * CB:(q + 1) * CB, :]).then_inc(s_xin, 16)
                with sp.Fori(0, NC // 2 - 2) as i:
                    for q in range(2):
                        hold(sp, s_in1, i * 2 + q + 1)
                        sp.dma_start(x_in[q][:], x_rows[:, bass.ds((i * 2 + q + 2) * CB, CB), :]).then_inc(s_xin, 16)
                    store(i)
                sp.wait_ge(s_in1, NC - 2)
                sp.dma_start(x_in[1][:, 0:CB - 1, :], x_rows[:, (NC - 1) * CB:NB - 1, :]).then_inc(s_xlast, 16)
                sp.wait_ge(s_xlast, 16)
                sp.dma_start(x_in[0][:], x_rows[:, (NC - 2) * CB:(NC - 1) * CB, :]).then_inc(s_xin, 16)
                sp.dma_start(x_in[1][0:N - (NB - 1) * P, CB - 1, :], x[(NB - 1) * P:N, :]).then_inc(s_xin, 16)
                store(NC // 2 - 2)
                store(NC // 2 - 1)
                sp.wait_ge(s_h2s, 16 * (NC + 1))
        st.close()

        st = ExitStack()
        HG = GT // 2
        r4 = sb(st, "r4", [P, T, 4])
        dl_now = sb(st, "dl_now1", [P, T])
        base_now = sb(st, "base_now1", [1, NG], I32)
        win = [sb(st, f"win{q}", [P, D]) for q in range(2)]
        srow = [sb(st, f"srow{q}", [P, GT * P], I16) for q in range(2)]
        equal = sb(st, "equal", [P, 2 * GT, P])
        place = sb(st, "place", [P, 2 * GT, W])
        mix = sb(st, "mix", [P, 2 * GT, P])
        val = sb(st, "val", [P, 2 * GT, RW])
        idx = [sb(st, f"idx{q}", [P, GT], I32) for q in range(2)]
        dup = sb(st, "dup", [P, 3, GT])
        ps_mix = [ps(st, f"ps_mix{h}", [P, HG, P]) for h in range(2)]
        ps_val = [ps(st, f"ps_val{h}", [P, HG, D]) for h in range(2)]
        ps_sum = [ps(st, f"ps_sum{q}", [P, GT, 4]) for q in range(2)]
        s_start = sem("layer1_started")
        s_srow = [sem(f"sources_loaded{q}") for q in range(2)]
        s_win1 = [sem(f"window_loaded{q}") for q in range(2)]
        s_built = sem("masks_built")
        s_sum = sem("source_sums_ready")
        s_mixp = [sem(f"mix_product{h}") for h in range(2)]
        s_mixc = [sem(f"mix_copied{h}") for h in range(2)]
        s_valp = [sem(f"value_product{h}") for h in range(2)]
        s_valc = [sem(f"value_copied{h}") for h in range(2)]
        s_dup = sem("index_chain")
        s_idx = sem("indices_ready")
        s_scat = [sem(f"scattered{k}") for k in range(NACC)]
        s_reuse = sem("half_reusable")
        s_trash = sem("trash_rows_ready")
        trash_i = sb(st, "trash_i", [P, 1], I32)
        nothing = sb(st, "nothing", [P, RW])
        block = nc.Block()
        with block:
            def buffers_scattered(eng, g):
                hold(eng, s_reuse, g + 1)

            @block.sync
            def _(sp):
                n_pass = pass_count(sp)
                with sp.Fori(0, n_pass) as k:
                    hold(sp, s_start, k + 1)
                    with sp.Fori(0, NG // 2) as i:
                        for q in range(2):
                            g = k * NG + i * 2 + q
                            base = sp.value_load(base_now[0:1, bass.ds(i * 2 + q, 1)], min_val=0, max_val=NP)
                            hold(sp, s_valp[1], g + 1)
                            sp.dma_start(srow[q][:], src16_flat[bass.ds((i * 2 + q) * GT * P, GT * P)
                                                                ].partition_broadcast(P)).then_inc(s_srow[q], 16)
                            sp.dma_start(win[q][:], h2_table[bass.ds(base, W), :]).then_inc(s_win1[q], 16)

            @block.vector
            def _(dve):
                link = Chain(dve, "columns_chain")
                dve.tensor_copy(r4[:, :, 0], w_c[:])
                dve.memset(r4[:, 0:E // P, 1], 1.0)
                link(dve.memset(r4[:, E // P:T, 1], 0.0))
                dve.memset(r4[0:E % P, E // P, 1:2], 1.0)
                link(dve.memset(r4[:, :, 2:4], 1.0))
                for k in (2, 3):
                    link(dve.tensor_scalar(r4[:, :, k], r4[:, :, k], con[:, C_U0 + k - 2:C_U0 + k - 1], None,
                                           ALU.mult))
                dve.tensor_copy(dl_now[:], dl[:])
                dve.memset(nothing[:], 0.0)
                dve.tensor_copy(trash_i[:], con[:, C_TRASH:C_TRASH + 1]).then_inc(s_trash, 1)
                dve.tensor_copy(base_now[:], base_i[:]).then_inc(s_start, 1)
                dve.wait_ge(s_start, 1)
                n_pass = pass_count(dve)
                with dve.Fori(0, n_pass) as k:
                    with dve.Fori(0, NG // 2) as i:
                        for q in range(2):
                            g = k * NG + i * 2 + q
                            hold(dve, s_srow[q], (k * (NG // 2) + i + 1) * 16)
                            for j in range(GT):
                                col = (i * 2 + q) * GT + j
                                slot = q * GT + j
                                dve.tensor_scalar(equal[:, slot, :], srow[q][:, j * P:(j + 1) * P],
                                                  src_c[:, bass.ds(col, 1)], None, ALU.is_equal)
                                bt = dve.tensor_scalar(place[:, slot, :], iota, dl_now[:, bass.ds(col, 1)],
                                                       w_c[:, bass.ds(col, 1)], ALU.is_equal, ALU.mult)
                            bt.then_inc(s_built, 1)
                            hold(dve, s_sum, g + 1)
                            sums = ps_sum[q]
                            own = src_c[:, bass.ds((i * 2 + q) * GT, GT)]
                            dve.tensor_scalar(dup[:, 0, :], sums[:, :, 2], con[:, C_T0:C_T0 + 1], None,
                                              ALU.is_ge).then_inc(s_dup, 1)
                            hold(dve, s_dup, g * 3 + 1)
                            dve.scalar_tensor_tensor(dup[:, 1, :], sums[:, :, 3], con[:, C_T1:C_T1 + 1],
                                                     dup[:, 0, :], ALU.is_ge, ALU.max).then_inc(s_dup, 1)
                            hold(dve, s_dup, g * 3 + 2)
                            dve.scalar_tensor_tensor(dup[:, 2, :], own, con[:, C_TRASH:C_TRASH + 1],
                                                     dup[:, 1, :], ALU.subtract, ALU.mult).then_inc(s_dup, 1)
                            buffers_scattered(dve, g)
                            hold(dve, s_dup, g * 3 + 3)
                            dve.tensor_copy(val[:, q * GT:(q + 1) * GT, D:RW], sums[:, :, 0:2])
                            dve.tensor_tensor(idx[q][:], own, dup[:, 2, :], ALU.subtract).then_inc(s_idx, 1)
                    dve.memset(r4[:, :, 0:2], 0.0)
                    dve.tensor_scalar(base_now[:], base_now[:], float(W), float(NP), ALU.add, ALU.min)
                    dve.tensor_scalar(dl_now[:], dl_now[:], -float(W), None, ALU.add).then_inc(s_start, 1)
                    hold(dve, s_start, k + 2)

            @block.tensor
            def _(pe):
                pe.sem_inc(s_valp[1], 2)
                n_pass = pass_count(pe)
                with pe.Fori(0, n_pass) as k:
                    with pe.Fori(0, NG // 2) as i:
                        for q in range(2):
                            g = k * NG + i * 2 + q
                            hold(pe, s_built, g + 1)
                            for j in range(GT):
                                mm = pe.matmul(ps_sum[q][:, j, :], equal[:, q * GT + j, :],
                                               r4[:, bass.ds((i * 2 + q) * GT + j, 1), :].rearrange(
                                                   "p a c -> p (a c)"), start=True, stop=True)
                            mm.then_inc(s_sum, 1)
                            for h in range(2):
                                for j in range(HG):
                                    slot = q * GT + h * HG + j
                                    mm = pe.matmul(ps_mix[h][:, j, :], place[:, slot, :], equal[:, slot, :],
                                                   start=True, stop=True)
                                mm.then_inc(s_mixp[h], 1)
                            hold(pe, s_win1[q], (k * (NG // 2) + i + 1) * 16)
                            for h in range(2):
                                hold(pe, s_mixc[h], g + 1)
                                hold(pe, s_valc[h], g + 1)
                                for j in range(HG):
                                    mm = pe.matmul(ps_val[h][:, j, :], mix[:, q * GT + h * HG + j, :], win[q][:],
                                                   start=True, stop=True)
                                mm.then_inc(s_valp[h], 1)

            @block.scalar
            def _(act):
                act.sem_inc(s_valc[0], 1)
                act.sem_inc(s_valc[1], 1)
                n_pass = pass_count(act)
                with act.Fori(0, n_pass) as k:
                    with act.Fori(0, NG // 2) as i:
                        for q in range(2):
                            g = k * NG + i * 2 + q
                            for h in range(2):
                                hold(act, s_mixp[h], g + 1)
                                lo = q * GT + h * HG
                                act.activation(mix[:, lo:lo + HG, :], ps_mix[h][:, :, :],
                                               ACT.Copy).then_inc(s_mixc[h], 1)
                            buffers_scattered(act, g)
                            for h in range(2):
                                hold(act, s_valp[h], g + (1 if h == 0 else 3))
                                lo = q * GT + h * HG
                                act.activation(val[:, lo:lo + HG, 0:D], ps_val[h][:, :, :],
                                               ACT.Copy).then_inc(s_valc[h], 1)

            @block.gpsimd
            def _(pool):
                pool.wait_ge(s_trash, 1)
                for a in range(NACC):
                    pool.indirect_dma_start(
                        acc[a], bass.IndirectOffsetOnAxis(ap=trash_i[:, 0:1], axis=0), nothing[:], None,
                        compute_op=ALU.add).then_inc(s_scat[a], 16)
                pool.sem_inc(s_reuse, 1)
                n_pass = pass_count(pool)
                with pool.Fori(0, n_pass) as k:
                    with pool.Fori(0, NG // 2) as i:
                        for q in range(2):
                            g = k * NG + i * 2 + q
                            hold(pool, s_idx, g + 1)
                            for j in range(GT):
                                if j % HG == 0:
                                    hold(pool, s_valc[j // HG], g + 2)
                                hold(pool, s_scat[j % NACC], g * 32 + 16 + 16 * (j // NACC))
                                pool.indirect_dma_start(
                                    acc[j % NACC], bass.IndirectOffsetOnAxis(ap=idx[q][:, j:j + 1], axis=0),
                                    val[:, q * GT + j, :], None, compute_op=ALU.add
                                ).then_inc(s_scat[j % NACC], 16)
                                if j == NACC - 1:
                                    pool.sem_inc(s_reuse, 1)
                for a in range(NACC):
                    hold(pool, s_scat[a], n_pass * (NG * 32) + 16)
        st.close()

        st = ExitStack()
        w_top = sb(st, "w_top", [P, D])
        w_bot = sb(st, "w_bot", [P, D])
        bias1_row = sb(st, "bias1_row", [P, D])
        part_acc = [sb(st, f"part_acc{q}", [P, NACC, CB, RW]) for q in range(2)]
        h2_in = [sb(st, f"h2_in{q}", [P, CB, D]) for q in range(2)]
        h2_w = [sb(st, f"h2_w{q}", [P, CB, D]) for q in range(2)]
        mean_cols = sb(st, "mean_cols", [P, 2, CW])
        scaled = [sb(st, f"scaled{q}", [P, CB, D]) for q in range(2)]
        ends2 = sb(st, "ends2", [P, CB, 2])
        cnt = sb(st, "cnt", [P, CB])
        per = [sb(st, f"per_count{q}", [P, CB]) for q in range(2)]
        ps_tt = [ps(st, f"ps_tt{k}", [P, 1024]) for k in range(2)]
        ps_o = [ps(st, f"ps_o{q}", [P, 1024]) for q in range(2)]
        s_w1 = sem("w1_loaded")
        s_part = [sem(f"sums_loaded{q}") for q in range(2)]
        s_fin = sem("final_chain")
        s_two = sem("mean_rows_ready")
        s_twot = sem("mean_rows_transposed")
        s_twoc = sem("mean_columns_copied")
        s_proj = sem("mean_projected")
        s_biased = sem("bias_added")
        s_scaled = sem("mean_scaled")
        s_res = sem("result_ready")
        s_out = sem("result_stored")
        block = nc.Block()
        with block:
            @block.sync
            def _(sp):
                sp.dma_start(bias1_row[:], bias1.partition_broadcast(P)).then_inc(s_w1, 16)
                sp.dma_start(w_top[:], w1[0:D, :]).then_inc(s_w1, 16)
                sp.dma_start(w_bot[:], w1[D:2 * D, :]).then_inc(s_w1, 16)
                views = [a[0:NP, :].rearrange("(b p) c -> p b c", p=P) for a in acc]
                table = h2_table[0:NP, :].rearrange("(b p) f -> p b f", p=P)
                results = out[0:(NB - 1) * P, :].rearrange("(b p) f -> p b f", p=P)

                def load(n, q):
                    for a in range(NACC):
                        sp.dma_start(part_acc[q][:, a, :, :], views[a][:, bass.ds(n * CB, CB), :]
                                     ).then_inc(s_part[q], 16)
                    sp.dma_start(h2_in[q][:], table[:, bass.ds(n * CB, CB), :]).then_inc(s_part[q], 16)

                def store(n):
                    hold(sp, s_res, n + 1)
                    sp.dma_start(results[:, bass.ds(n * CB, CB), :],
                                 agg[:, bass.ds(n * CW, CW)].rearrange("p (b f) -> p b f", f=D)).then_inc(s_out, 16)

                for q in range(2):
                    load(q, q)
                with sp.Fori(0, NC // 2 - 1) as i:
                    for q in range(2):
                        hold(sp, s_twot, i * 2 + q + 1)
                        load(i * 2 + q + 2, q)
                        store(i * 2 + q)
                store(NC - 2)
                sp.wait_ge(s_res, NC)
                last = agg[:, (NC - 1) * CW:NC * CW].rearrange("p (b f) -> p b f", f=D)
                sp.dma_start(results[:, (NC - 1) * CB:NB - 1, :], last[:, 0:CB - 1, :]).then_inc(s_out, 16)
                sp.dma_start(out[(NB - 1) * P:N, :], last[0:N - (NB - 1) * P, CB - 1, :]).then_inc(s_out, 16)
                sp.wait_ge(s_out, 16 * (NC + 1))

            @block.gpsimd
            def _(pool):
                pool.wait_ge(s_w1, 48)
                with pool.Fori(0, NC) as n:
                    here = agg[:, bass.ds(n * CW, CW)].rearrange("p (b f) -> p b f", f=D)
                    pool.tensor_tensor(here, here, bias1_row[:, :].unsqueeze(1).broadcast_to([P, CB, D]),
                                       ALU.add).then_inc(s_biased, 1)

            @block.vector
            def _(dve):
                def prepare(n, q, turn):
                    def link(instruction, k):
                        instruction.then_inc(s_fin, 1)
                        hold(dve, s_fin, n * 4 + k)

                    hold(dve, s_part[q], turn * 80 + 80)
                    flat = part_acc[q][:, :, :, :].rearrange("p a b c -> p a (b c)")
                    link(dve.tensor_tensor(flat[:, 0:2, :], flat[:, 0:2, :], flat[:, 2:4, :], ALU.add), 1)
                    link(dve.tensor_tensor(ends2[:], part_acc[q][:, 0, :, D:RW], part_acc[q][:, 1, :, D:RW],
                                           ALU.add), 2)
                    dve.tensor_tensor(h2_w[q][:], h2_in[q][:],
                                      ends2[:, :, 0].unsqueeze(2).broadcast_to([P, CB, D]),
                                      ALU.mult).then_inc(s_two, 1)
                    link(dve.tensor_scalar(cnt[:], ends2[:, :, 1], 1.0, None, ALU.max), 3)
                    link(dve.reciprocal(per[q][:], cnt[:]), 4)

                def finish(n, q):
                    hold(dve, s_proj, n + 1)
                    dve.tensor_tensor(scaled[q][:], ps_o[q][:, 0:CW].rearrange("p (b f) -> p b f", f=D),
                                      per[q][:, :].unsqueeze(2).broadcast_to([P, CB, D]),
                                      ALU.mult).then_inc(s_scaled, 1)
                    hold(dve, s_biased, n + 1)
                    hold(dve, s_scaled, n + 1)
                    here = agg[:, bass.ds(n * CW, CW)].rearrange("p (b f) -> p b f", f=D)
                    dve.tensor_tensor(here, here, scaled[q][:], ALU.add).then_inc(s_res, 1)

                prepare(0, 0, 0)
                with dve.Fori(0, NC // 2 - 1) as i:
                    prepare(i * 2 + 1, 1, i)
                    finish(i * 2, 0)
                    prepare(i * 2 + 2, 0, i + 1)
                    finish(i * 2 + 1, 1)
                prepare(NC - 1, 1, NC // 2 - 1)
                finish(NC - 2, 0)
                finish(NC - 1, 1)

            @block.tensor
            def _(pe):
                pe.wait_ge(s_w1, 48)
                with pe.Fori(0, NC // 2) as i:
                    for q in range(2):
                        n = i * 2 + q
                        hold(pe, s_two, n + 1)
                        for b in range(CB):
                            pe.transpose(ps_tt[0][:, b * P:(b + 1) * P], h2_w[q][:, b, :], ident)
                            for a in range(2):
                                tp = pe.matmul(ps_tt[1][:, b * P:(b + 1) * P], part_acc[q][:, a, b, 0:D], ident,
                                               start=(a == 0), stop=(a == 1))
                        tp.then_inc(s_twot, 1)
                        hold(pe, s_twoc, n + 1)
                        for b in range(CB):
                            pe.matmul(ps_o[q][:, b * P:(b + 1) * P], mean_cols[:, 0, b * P:(b + 1) * P], w_top[:],
                                      start=True, stop=False)
                            mm = pe.matmul(ps_o[q][:, b * P:(b + 1) * P], mean_cols[:, 1, b * P:(b + 1) * P], w_bot[:],
                                           start=False, stop=True)
                        mm.then_inc(s_proj, 1)

            @block.scalar
            def _(act):
                with act.Fori(0, NC) as n:
                    hold(act, s_twot, n + 1)
                    act.activation(mean_cols[:, 0, :], ps_tt[0][:, 0:CW], ACT.Copy)
                    act.activation(mean_cols[:, 1, :], ps_tt[1][:, 0:CW], ACT.Copy).then_inc(s_twoc, 1)
        st.close()
        agg_stack.close()
        to_layer1.close()


def kernel(x, src, dst, edge_weight1, L0_gnn_W, L0_gnn_a_src, L0_gnn_a_dst, L0_gnn_bias,
           L1_gnn_weight, L1_gnn_bias):
    import numpy as _np
    import concourse.bacc as _bacc
    from concourse.bass_utils import run_bass_kernel_spmd as _run

    nc = _bacc.Bacc("TRN2", target_bir_lowering=False, num_devices=1)
    arrays = {
        "x": _np.asarray(x), "src": _np.asarray(src), "dst": _np.asarray(dst),
        "weight": _np.asarray(edge_weight1).reshape(E), "w0": _np.asarray(L0_gnn_W),
        "a_src": _np.asarray(L0_gnn_a_src), "a_dst": _np.asarray(L0_gnn_a_dst),
        "bias0": _np.asarray(L0_gnn_bias), "w1": _np.asarray(L1_gnn_weight),
        "bias1": _np.asarray(L1_gnn_bias), "consts": shape_constants(),
    }
    args = [nc.dram_tensor(n, a.shape, mybir.dt.from_np(a.dtype), kind="ExternalInput").ap()
            for n, a in arrays.items()]
    out = nc.dram_tensor("out", (N, D), F32, kind="ExternalOutput").ap()
    build(nc, *args, out)
    got = _run(nc, [arrays], core_ids=[0])
    return got.results[0]["out"]
```
